# Optimizing a Trainium2 kernel written in Bass

```python
import numpy as np
import jax
import jax.numpy as jnp

def _softmax(x, axis=-1):
    return jax.nn.softmax(x, axis=axis)

def _gelu(x):
    return jax.nn.gelu(x, approximate=True)

def _silu(x):
    return jax.nn.silu(x)

def _sigmoid(x):
    return jax.nn.sigmoid(x)

def _layernorm(x, axis=-1, eps=1e-05):
    m = jnp.mean(x, axis=axis, keepdims=True)
    v = jnp.var(x, axis=axis, keepdims=True)
    return (x - m) / jnp.sqrt(v + eps)

def _scatter_add(tgt, idx, src, axis=0):
    return tgt.at[idx].add(src)

def _segment_sum(src, seg, n):
    return jax.ops.segment_sum(src, seg, n)
kernel_name = 'mk_dlrm_tower_d1_rec_r8_f91a1b'

def setup_inputs(seed: int=0):
    np.random.seed(seed)
    _w = jnp.asarray

    def _rec_inputs():
        import jax
        import jax.numpy as jnp
        _tk = jax.random.key(seed)
        dense_ctx = jax.random.normal(jax.random.fold_in(_tk, 190), (2048, 16), jnp.float32)
        ids = jnp.stack([jax.random.randint(jax.random.fold_in(_tk, 200 + f), (2048,), 0, v, jnp.int32) for f, v in enumerate([1000, 1000, 125000, 12500, 12500, 1000, 125000, 12500, 125000, 12500, 1000, 1250, 125000, 125000, 1000, 12500, 125000, 1000, 1250, 1250, 125000, 125000, 12500, 12500, 1000, 1000, 125000, 1250, 125000, 125000, 12500, 12500, 1000, 125000, 1000, 125000, 12500, 1000, 12500])], axis=1)
        tbl_0 = 0.05 * jax.random.normal(jax.random.fold_in(_tk, 500 + 0), (1000, 16), jnp.float32)
        tbl_1 = 0.05 * jax.random.normal(jax.random.fold_in(_tk, 500 + 1), (1000, 16), jnp.float32)
        tbl_2 = 0.05 * jax.random.normal(jax.random.fold_in(_tk, 500 + 2), (125000, 16), jnp.float32)
        tbl_3 = 0.05 * jax.random.normal(jax.random.fold_in(_tk, 500 + 3), (12500, 16), jnp.float32)
        tbl_4 = 0.05 * jax.random.normal(jax.random.fold_in(_tk, 500 + 4), (12500, 16), jnp.float32)
        tbl_5 = 0.05 * jax.random.normal(jax.random.fold_in(_tk, 500 + 5), (1000, 16), jnp.float32)
        tbl_6 = 0.05 * jax.random.normal(jax.random.fold_in(_tk, 500 + 6), (125000, 16), jnp.float32)
        tbl_7 = 0.05 * jax.random.normal(jax.random.fold_in(_tk, 500 + 7), (12500, 16), jnp.float32)
        tbl_8 = 0.05 * jax.random.normal(jax.random.fold_in(_tk, 500 + 8), (125000, 16), jnp.float32)
        tbl_9 = 0.05 * jax.random.normal(jax.random.fold_in(_tk, 500 + 9), (12500, 16), jnp.float32)
        tbl_10 = 0.05 * jax.random.normal(jax.random.fold_in(_tk, 500 + 10), (1000, 16), jnp.float32)
        tbl_11 = 0.05 * jax.random.normal(jax.random.fold_in(_tk, 500 + 11), (1250, 16), jnp.float32)
        tbl_12 = 0.05 * jax.random.normal(jax.random.fold_in(_tk, 500 + 12), (125000, 16), jnp.float32)
        tbl_13 = 0.05 * jax.random.normal(jax.random.fold_in(_tk, 500 + 13), (125000, 16), jnp.float32)
        tbl_14 = 0.05 * jax.random.normal(jax.random.fold_in(_tk, 500 + 14), (1000, 16), jnp.float32)
        tbl_15 = 0.05 * jax.random.normal(jax.random.fold_in(_tk, 500 + 15), (12500, 16), jnp.float32)
        tbl_16 = 0.05 * jax.random.normal(jax.random.fold_in(_tk, 500 + 16), (125000, 16), jnp.float32)
        tbl_17 = 0.05 * jax.random.normal(jax.random.fold_in(_tk, 500 + 17), (1000, 16), jnp.float32)
        tbl_18 = 0.05 * jax.random.normal(jax.random.fold_in(_tk, 500 + 18), (1250, 16), jnp.float32)
        tbl_19 = 0.05 * jax.random.normal(jax.random.fold_in(_tk, 500 + 19), (1250, 16), jnp.float32)
        tbl_20 = 0.05 * jax.random.normal(jax.random.fold_in(_tk, 500 + 20), (125000, 16), jnp.float32)
        tbl_21 = 0.05 * jax.random.normal(jax.random.fold_in(_tk, 500 + 21), (125000, 16), jnp.float32)
        tbl_22 = 0.05 * jax.random.normal(jax.random.fold_in(_tk, 500 + 22), (12500, 16), jnp.float32)
        tbl_23 = 0.05 * jax.random.normal(jax.random.fold_in(_tk, 500 + 23), (12500, 16), jnp.float32)
        tbl_24 = 0.05 * jax.random.normal(jax.random.fold_in(_tk, 500 + 24), (1000, 16), jnp.float32)
        tbl_25 = 0.05 * jax.random.normal(jax.random.fold_in(_tk, 500 + 25), (1000, 16), jnp.float32)
        tbl_26 = 0.05 * jax.random.normal(jax.random.fold_in(_tk, 500 + 26), (125000, 16), jnp.float32)
        tbl_27 = 0.05 * jax.random.normal(jax.random.fold_in(_tk, 500 + 27), (1250, 16), jnp.float32)
        tbl_28 = 0.05 * jax.random.normal(jax.random.fold_in(_tk, 500 + 28), (125000, 16), jnp.float32)
        tbl_29 = 0.05 * jax.random.normal(jax.random.fold_in(_tk, 500 + 29), (125000, 16), jnp.float32)
        tbl_30 = 0.05 * jax.random.normal(jax.random.fold_in(_tk, 500 + 30), (12500, 16), jnp.float32)
        tbl_31 = 0.05 * jax.random.normal(jax.random.fold_in(_tk, 500 + 31), (12500, 16), jnp.float32)
        tbl_32 = 0.05 * jax.random.normal(jax.random.fold_in(_tk, 500 + 32), (1000, 16), jnp.float32)
        tbl_33 = 0.05 * jax.random.normal(jax.random.fold_in(_tk, 500 + 33), (125000, 16), jnp.float32)
        tbl_34 = 0.05 * jax.random.normal(jax.random.fold_in(_tk, 500 + 34), (1000, 16), jnp.float32)
        tbl_35 = 0.05 * jax.random.normal(jax.random.fold_in(_tk, 500 + 35), (125000, 16), jnp.float32)
        tbl_36 = 0.05 * jax.random.normal(jax.random.fold_in(_tk, 500 + 36), (12500, 16), jnp.float32)
        tbl_37 = 0.05 * jax.random.normal(jax.random.fold_in(_tk, 500 + 37), (1000, 16), jnp.float32)
        tbl_38 = 0.05 * jax.random.normal(jax.random.fold_in(_tk, 500 + 38), (12500, 16), jnp.float32)
        _rk = jax.random.fold_in(_tk, 7)
        W_top1 = 0.0606339 * jax.random.normal(jax.random.fold_in(_tk, 801), (272, 512), jnp.float32)
        W_top2 = 0.0441942 * jax.random.normal(jax.random.fold_in(_tk, 802), (512, 256), jnp.float32)
        W_top3 = 0.0625 * jax.random.normal(jax.random.fold_in(_tk, 803), (256, 1), jnp.float32)
        b_top1 = jnp.zeros((512,), jnp.float32)
        b_top2 = jnp.zeros((256,), jnp.float32)
        return (dense_ctx, ids, tbl_0, tbl_1, tbl_2, tbl_3, tbl_4, tbl_5, tbl_6, tbl_7, tbl_8, tbl_9, tbl_10, tbl_11, tbl_12, tbl_13, tbl_14, tbl_15, tbl_16, tbl_17, tbl_18, tbl_19, tbl_20, tbl_21, tbl_22, tbl_23, tbl_24, tbl_25, tbl_26, tbl_27, tbl_28, tbl_29, tbl_30, tbl_31, tbl_32, tbl_33, tbl_34, tbl_35, tbl_36, tbl_37, tbl_38, W_top1, b_top1, W_top2, b_top2, W_top3)
    dense_ctx, ids, tbl_0, tbl_1, tbl_2, tbl_3, tbl_4, tbl_5, tbl_6, tbl_7, tbl_8, tbl_9, tbl_10, tbl_11, tbl_12, tbl_13, tbl_14, tbl_15, tbl_16, tbl_17, tbl_18, tbl_19, tbl_20, tbl_21, tbl_22, tbl_23, tbl_24, tbl_25, tbl_26, tbl_27, tbl_28, tbl_29, tbl_30, tbl_31, tbl_32, tbl_33, tbl_34, tbl_35, tbl_36, tbl_37, tbl_38, W_top1, b_top1, W_top2, b_top2, W_top3 = _rec_inputs()

    def _L0_rec_setup():
        import jax, jax.numpy as jnp
        import numpy as np
        NUM_FIELD = 39
        CIN_SIZE = [128, 128]
        EMBED_DIM = 16
        BATCH = 256
        key = jax.random.key(seed)
        k1, k2, k3 = jax.random.split(key, 3)
        x_emb = jax.random.normal(k1, (BATCH, NUM_FIELD, EMBED_DIM), dtype=jnp.float32)
        W0 = jax.random.normal(k2, (CIN_SIZE[0], NUM_FIELD * NUM_FIELD), dtype=jnp.float32) * 0.02
        W1 = jax.random.normal(k3, (CIN_SIZE[1], CIN_SIZE[0] * NUM_FIELD), dtype=jnp.float32) * 0.02
        return {'x_emb': x_emb, 'W0': W0, 'W1': W1}
    _L0_rec_all = _L0_rec_setup()
    _L0_rec_in = {k: v for k, v in _L0_rec_all.items() if k in ('W0', 'W1')}
    del _L0_rec_all
    return {'dense_ctx': dense_ctx, 'ids': ids, 'tbl_0': tbl_0, 'tbl_1': tbl_1, 'tbl_2': tbl_2, 'tbl_3': tbl_3, 'tbl_4': tbl_4, 'tbl_5': tbl_5, 'tbl_6': tbl_6, 'tbl_7': tbl_7, 'tbl_8': tbl_8, 'tbl_9': tbl_9, 'tbl_10': tbl_10, 'tbl_11': tbl_11, 'tbl_12': tbl_12, 'tbl_13': tbl_13, 'tbl_14': tbl_14, 'tbl_15': tbl_15, 'tbl_16': tbl_16, 'tbl_17': tbl_17, 'tbl_18': tbl_18, 'tbl_19': tbl_19, 'tbl_20': tbl_20, 'tbl_21': tbl_21, 'tbl_22': tbl_22, 'tbl_23': tbl_23, 'tbl_24': tbl_24, 'tbl_25': tbl_25, 'tbl_26': tbl_26, 'tbl_27': tbl_27, 'tbl_28': tbl_28, 'tbl_29': tbl_29, 'tbl_30': tbl_30, 'tbl_31': tbl_31, 'tbl_32': tbl_32, 'tbl_33': tbl_33, 'tbl_34': tbl_34, 'tbl_35': tbl_35, 'tbl_36': tbl_36, 'tbl_37': tbl_37, 'tbl_38': tbl_38, 'W_top1': W_top1, 'b_top1': b_top1, 'W_top2': W_top2, 'b_top2': b_top2, 'W_top3': W_top3, 'L0_rec_W0': _L0_rec_in['W0'], 'L0_rec_W1': _L0_rec_in['W1']}

def reference(dense_ctx, ids, tbl_0, tbl_1, tbl_2, tbl_3, tbl_4, tbl_5, tbl_6, tbl_7, tbl_8, tbl_9, tbl_10, tbl_11, tbl_12, tbl_13, tbl_14, tbl_15, tbl_16, tbl_17, tbl_18, tbl_19, tbl_20, tbl_21, tbl_22, tbl_23, tbl_24, tbl_25, tbl_26, tbl_27, tbl_28, tbl_29, tbl_30, tbl_31, tbl_32, tbl_33, tbl_34, tbl_35, tbl_36, tbl_37, tbl_38, W_top1, b_top1, W_top2, b_top2, W_top3, L0_rec_W0, L0_rec_W1):
    import jax
    import jax.numpy as jnp

    def _L0_rec_ref(x_emb, W0, W1):
        import jax, jax.numpy as jnp
        import numpy as np
        NUM_FIELD = 39
        CIN_SIZE = [128, 128]
        EMBED_DIM = 16
        BATCH = 256
        B, F, D = x_emb.shape
        x = x_emb
        outs = []
        for W in (W0, W1):
            last = x.shape[1]
            inter = (x[:, :, None, :] * x_emb[:, None, :, :]).reshape(B, last * F, D)
            x = jnp.einsum('bid,hi->bhd', inter, W)
            outs.append(x.sum(axis=-1))
        return jnp.concatenate(outs, axis=-1)
    e = jnp.stack([tbl_0[ids[:, 0]], tbl_1[ids[:, 1]], tbl_2[ids[:, 2]], tbl_3[ids[:, 3]], tbl_4[ids[:, 4]], tbl_5[ids[:, 5]], tbl_6[ids[:, 6]], tbl_7[ids[:, 7]], tbl_8[ids[:, 8]], tbl_9[ids[:, 9]], tbl_10[ids[:, 10]], tbl_11[ids[:, 11]], tbl_12[ids[:, 12]], tbl_13[ids[:, 13]], tbl_14[ids[:, 14]], tbl_15[ids[:, 15]], tbl_16[ids[:, 16]], tbl_17[ids[:, 17]], tbl_18[ids[:, 18]], tbl_19[ids[:, 19]], tbl_20[ids[:, 20]], tbl_21[ids[:, 21]], tbl_22[ids[:, 22]], tbl_23[ids[:, 23]], tbl_24[ids[:, 24]], tbl_25[ids[:, 25]], tbl_26[ids[:, 26]], tbl_27[ids[:, 27]], tbl_28[ids[:, 28]], tbl_29[ids[:, 29]], tbl_30[ids[:, 30]], tbl_31[ids[:, 31]], tbl_32[ids[:, 32]], tbl_33[ids[:, 33]], tbl_34[ids[:, 34]], tbl_35[ids[:, 35]], tbl_36[ids[:, 36]], tbl_37[ids[:, 37]], tbl_38[ids[:, 38]]], axis=1)
    z = _L0_rec_ref(e, L0_rec_W0, L0_rec_W1)
    z = z.reshape(z.shape[0], -1)
    h = jnp.concatenate([z, dense_ctx], axis=1)
    h = jnp.maximum(h @ W_top1 + b_top1, 0.0)
    h = jnp.maximum(h @ W_top2 + b_top2, 0.0)
    y = h @ W_top3
    return y

_drawn_inputs = setup_inputs


def setup_inputs(seed=0):
    import zlib

    import numpy as np

    out = dict(_drawn_inputs(seed))
    spreads = {'b_top1': (0.0, 0.1), 'b_top2': (0.0, 0.1)}
    factors = {'tbl_0': 8.0,
     'tbl_1': 8.0,
     'tbl_2': 8.0,
     'tbl_3': 8.0,
     'tbl_4': 8.0,
     'tbl_5': 8.0,
     'tbl_6': 8.0,
     'tbl_7': 8.0,
     'tbl_8': 8.0,
     'tbl_9': 8.0,
     'tbl_10': 8.0,
     'tbl_11': 8.0,
     'tbl_12': 8.0,
     'tbl_13': 8.0,
     'tbl_14': 8.0,
     'tbl_15': 8.0,
     'tbl_16': 8.0,
     'tbl_17': 8.0,
     'tbl_18': 8.0,
     'tbl_19': 8.0,
     'tbl_20': 8.0,
     'tbl_21': 8.0,
     'tbl_22': 8.0,
     'tbl_23': 8.0,
     'tbl_24': 8.0,
     'tbl_25': 8.0,
     'tbl_26': 8.0,
     'tbl_27': 8.0,
     'tbl_28': 8.0,
     'tbl_29': 8.0,
     'tbl_30': 8.0,
     'tbl_31': 8.0,
     'tbl_32': 8.0,
     'tbl_33': 8.0,
     'tbl_34': 8.0,
     'tbl_35': 8.0,
     'tbl_36': 8.0,
     'tbl_37': 8.0,
     'tbl_38': 8.0,
     'L0_rec_W1': 8.0}
    for name, (base, spread) in spreads.items():
        noise = np.random.default_rng([zlib.crc32(name.encode()), seed]).standard_normal(out[name].shape)
        drawn = base * np.exp(spread * noise) if base else spread * noise
        out[name] = jnp.asarray(drawn.astype(out[name].dtype))
    for name, factor in factors.items():
        out[name] = (out[name] * factor).astype(out[name].dtype)
    return out
```

```python
import numpy as np
import concourse.bass as bass
from concourse import mybir
from contextlib import ExitStack

F = 39
D = 16
B = 2048
H = 128
SHIFTS = (F + 1) // 2
PER_TILE = 3
KT = -(-SHIFTS // PER_TILE)
ROWS = PER_TILE * F
TB = 128
TILES = B // TB
CB = 32
COLS = CB * D
CPT = TB // CB
TPI = 2
CPI = CPT * TPI
NB = TB * TPI
ITERS = B // NB
Q = COLS // 128
FO = F + 1
H1, H2 = 512, 256
M1, M2 = H1 // 128, H2 // 128
PRING = 4


def after(engine, semaphore, value):
    if isinstance(value, int) and value <= 0:
        return
    engine.wait_ge(semaphore, value)


def rows_of(k):
    return min(PER_TILE, SHIFTS - k * PER_TILE) * F


def cin_tower(nc, dense_t, ids, tables, w_top1, b_top1, w_top2, b_top2, w_top3, w0, w1,
              select, pair_mask, identity, out):
    f32, bf16, i32 = mybir.dt.float32, mybir.dt.bfloat16, mybir.dt.int32
    ALU = mybir.AluOpType
    ACT = mybir.ActivationFunctionType
    ctx = ExitStack()
    with ctx:
        def sb(name, shape, dt=f32):
            return ctx.enter_context(nc.sbuf_tensor(name, shape, dt))

        def ps(name, shape, dt=f32):
            return ctx.enter_context(nc.psum_tensor(name, shape, dt))

        def sem(name):
            return ctx.enter_context(nc.semaphore(name))

        select_f = sb("select_f", [ROWS, ROWS + SHIFTS * F])
        select_b = sb("select_b", [ROWS, ROWS + SHIFTS * F], bf16)
        mask = sb("mask", [128, 2])
        ident = sb("ident", [128, 128])
        ident_b = sb("ident_b", [128, 128], bf16)
        w0_both = sb("w0_both", [ROWS, 2, KT, H])
        w0T = sb("w0T", [ROWS, KT, H])
        w1T = sb("w1T", [H, F, H])
        wt1_cin = sb("wt1_cin", [128, 2, H1])
        wt1_dense = sb("wt1_dense", [D, H1])
        wt2 = sb("wt2", [128, M1, H2])
        wt3 = sb("wt3", [128, M2])
        bias1 = sb("bias1", [128, M1])
        bias2 = sb("bias2", [128, M2])
        denseT = sb("denseT", [D, B])
        ids_sb = [sb(f"ids_sb{n}", [128, F], i32) for n in range(2)]
        e_rows = [sb(f"e_rows{n}", [128, F * D]) for n in range(2)]
        e_rest = sb("e_rest", [128, D, F])
        e_parts = [sb(f"e_parts{n}", [128, D, 3, F], bf16) for n in range(2)]
        eT = [sb(f"eT{n}", [ROWS, TB, D], bf16) for n in range(2)]
        e3 = [sb(f"e3_{n}", [ROWS, COLS]) for n in range(2)]
        products = sb("products", [ROWS, PRING, COLS])
        x1 = sb("x1", [H, COLS])
        x1T = sb("x1T", [128, Q, H])
        e_diag = sb("e_diag", [128, Q, 2, FO])
        G = sb("G", [H, FO, NB])
        z2 = sb("z2", [H, NB])
        dense_now = sb("dense_now", [D, NB])
        h1 = sb("h1", [128, M1, NB])
        h2 = sb("h2", [128, M2, NB])
        y = sb("y", [1, B])

        rep_ps = [ps(f"rep_ps{n}", [128, COLS]) for n in range(2)]
        x1_ps = ps("x1_ps", [H, COLS])
        aux_ps = ps("aux_ps", [128, 512])
        g_ps = [ps(f"g_ps{n}", [128, 512]) for n in range(4)]

        consts_loaded = sem("consts_loaded")
        w0_loaded = sem("w0_loaded")
        w1_loaded = sem("w1_loaded")
        dense_loaded = sem("dense_loaded")
        mlp_loaded = sem("mlp_loaded")
        consts_cast = sem("consts_cast")
        w0_summed = sem("w0_summed")
        ids_loaded = [sem(f"ids_loaded{n}") for n in range(2)]
        gathered = [sem(f"gathered{n}") for n in range(2)]
        tiles_begun = sem("tiles_begun")
        split_step = sem("split_step")
        split_done = sem("split_done")
        eT_in_ps = sem("eT_in_ps")
        eT_ready = sem("eT_ready")
        e3_in_ps = sem("e3_in_ps")
        e3_ready = sem("e3_ready")
        rep_in_ps = sem("rep_in_ps")
        product_ready = sem("product_ready")
        x1_in_ps = sem("x1_in_ps")
        x1_ready = sem("x1_ready")
        e_in_ps = sem("e_in_ps")
        e_diag_ready = sem("e_diag_ready")
        x1T_in_ps = sem("x1T_in_ps")
        x1T_ready = sem("x1T_ready")
        g_in_ps = sem("g_in_ps")
        g_ready_act = sem("g_ready_act")
        g_ready_dve = sem("g_ready_dve")
        z2_in_ps = sem("z2_in_ps")
        z2_ready = sem("z2_ready")
        dense_ready = sem("dense_ready")
        h1_in_ps = sem("h1_in_ps")
        h1_ready = sem("h1_ready")
        h2_in_ps = sem("h2_in_ps")
        h2_ready = sem("h2_ready")
        y_in_ps = sem("y_in_ps")
        y_ready = sem("y_ready")
        y_stored = sem("y_stored")

        block = ctx.enter_context(nc.Block())

        @block.sync
        def _(sp):
            sp.dma_start(ids_sb[0][:, :], ids[0:TB, :]).then_inc(ids_loaded[0], 16)
            sp.dma_start(ids_sb[1][:, :], ids[TB:2 * TB, :]).then_inc(ids_loaded[1], 16)
            sp.dma_start(ident[:, :], identity).then_inc(consts_loaded, 16)
            sp.dma_start(select_f[:, :], select).then_inc(consts_loaded, 16)
            sp.dma_start(mask[:, :], pair_mask).then_inc(consts_loaded, 16)
            sp.dma_start(w0_both[:, :, :, :], w0).then_inc(w0_loaded, 16)
            sp.dma_start(denseT[:, :], dense_t).then_inc(dense_loaded, 16)
            sp.dma_start(w1T[:, :, :], w1).then_inc(w1_loaded, 16)
            sp.dma_start(wt1_cin[:, :, :], w_top1[0:2 * H, :].rearrange("(k p) n -> p k n", p=128)).then_inc(mlp_loaded, 16)
            sp.dma_start(wt1_dense[:, :], w_top1[2 * H:2 * H + D, :]).then_inc(mlp_loaded, 16)
            sp.dma_start(wt2[:, :, :], w_top2.rearrange("(k p) n -> p k n", p=128)).then_inc(mlp_loaded, 16)
            sp.dma_start(wt3[:, :], w_top3).then_inc(mlp_loaded, 16)
            sp.dma_start(bias1[:, :], b_top1).then_inc(mlp_loaded, 16)
            sp.dma_start(bias2[:, :], b_top2).then_inc(mlp_loaded, 16)
            with sp.Fori(1, ITERS) as it:
                for slot in range(TPI):
                    sp.wait_ge(gathered[slot], it * (16 * F))
                    sp.dma_start(ids_sb[slot][:, :], ids[bass.ds(it * NB + slot * TB, TB), :]).then_inc(ids_loaded[slot], 16)
            sp.wait_ge(y_ready, ITERS)
            sp.dma_start(out.rearrange("b o -> o b"), y[:, :]).then_inc(y_stored, 16)
            sp.wait_ge(y_stored, 16)

        @block.gpsimd
        def _(pool):
            def body(it):
                for slot in range(TPI):
                    pool.wait_ge(ids_loaded[slot], it * 16 + 16)
                    after(pool, split_done, (it - 1) * TPI + slot + 1)
                    pool.sem_inc(tiles_begun, 1)
                    for f in range(F):
                        nc.gpsimd.indirect_dma_start(
                            out=e_rows[slot][:, f * D:(f + 1) * D], out_offset=None, in_=tables[f],
                            in_offset=bass.IndirectOffsetOnAxis(ap=ids_sb[slot][:, f:f + 1], axis=0),
                        ).then_inc(gathered[slot], 16)

            body(0)
            with pool.Fori(1, ITERS) as it:
                body(it)

        @block.tensor
        def _(pe):
            pe.wait_ge(consts_cast, 2)
            pe.wait_ge(w0_summed, 2)
            pe.wait_ge(w1_loaded, 16)
            pe.wait_ge(mlp_loaded, 6 * 16)

            def columns(c):
                return eT[c // CPT][:, :, :].rearrange("r b d -> r (b d)")[:, c % CPT * COLS:(c % CPT + 1) * COLS]

            def transpose_e(it, slot):
                pe.wait_ge(split_done, it * TPI + slot + 1)
                for half in range(2):
                    if half == 0:
                        after(pe, x1T_ready, it * CPI + (0 if slot == 0 else 2))
                    else:
                        pe.wait_ge(eT_ready, it * 2 * TPI + slot * 2 + 1)
                    halves = aux_ps[:, :].bitcast(bf16).rearrange("r (d b) -> r d b", b=TB)
                    for d in range(D // 2):
                        last = nc.tensor.transpose(halves[0:ROWS, d, :], e_parts[slot][:, half * 8 + d, :, :].rearrange("b q f -> b (q f)"), ident_b[:, :])
                    last.then_inc(eT_in_ps, 1)

            def replicate_e3(it, c):
                g = it * CPI + c
                after(pe, product_ready, (g - 1) * KT + KT - 1)
                nc.tensor.matmul(rep_ps[0][0:ROWS, :], select_b[:, 0:ROWS], columns(c), start=True, stop=True).then_inc(e3_in_ps, 1)

            def replicate(it, c, k):
                g = it * CPI + c
                if k == 1:
                    pe.wait_ge(e3_ready, g + 1)
                else:
                    after(pe, product_ready, g * KT + k - 1 if k else g * KT)
                rows = rows_of(k)
                nc.tensor.matmul(rep_ps[(k + 1) % 2][0:rows, :], select_b[:, ROWS + k * ROWS:ROWS + k * ROWS + rows],
                                 columns(c), start=True, stop=True).then_inc(rep_in_ps, 1)

            def tail_e(it, c):
                g = it * CPI + c
                if c == 0:
                    pe.wait_ge(eT_ready, it * 2 * TPI + 2)
                elif c == 2:
                    pe.wait_ge(eT_ready, it * 2 * TPI + 4)
                else:
                    after(pe, x1T_ready, g)
                for q in range(Q):
                    last = nc.tensor.matmul(aux_ps[:, q * FO:q * FO + F], columns(c)[:, q * 128:(q + 1) * 128],
                                            select_b[:, 0:F], start=True, stop=True)
                last.then_inc(e_in_ps, 1)

            def tail_x1T(it, c):
                g = it * CPI + c
                pe.wait_ge(e_diag_ready, g + 1)
                pe.wait_ge(x1_ready, g + 1)
                for q in range(Q):
                    last = nc.tensor.transpose(aux_ps[:, q * 128:(q + 1) * 128], x1[:, q * 128:(q + 1) * 128], ident[:, :])
                last.then_inc(x1T_in_ps, 1)

            def tail_g(it, c):
                g = it * CPI + c
                pe.wait_ge(x1T_ready, g + 1)
                after(pe, g_ready_act, 2 * g)
                after(pe, g_ready_dve, 2 * g)
                if c == 0:
                    after(pe, y_ready, it)
                for q in range(Q):
                    for r in range(4):
                        last = nc.tensor.matmul(g_ps[r][:, q * 2 * FO:(q + 1) * 2 * FO], x1T[32 * r:32 * (r + 1), q, :],
                                                e_diag[32 * r:32 * (r + 1), q, :, :].rearrange("p b f -> p (b f)"),
                                                start=True, stop=True)
                last.then_inc(g_in_ps, 1)

            def chunk(it, c):
                g = it * CPI + c
                if c == 0:
                    transpose_e(it, 0)
                    pe.wait_ge(eT_ready, it * 2 * TPI + 2)
                    replicate_e3(it, 0)
                    replicate(it, 0, 0)
                    replicate(it, 0, 1)
                for k in range(KT):
                    if k + 2 < KT:
                        replicate(it, c, k + 2)
                    elif k + 2 == KT and c + 1 < CPI:
                        if c + 1 == CPT:
                            pe.wait_ge(eT_ready, it * 2 * TPI + 4)
                        replicate_e3(it, c + 1)
                    elif c + 1 < CPI:
                        replicate(it, c + 1, 0)
                    if k == 0:
                        after(pe, x1_ready, g)
                    pe.wait_ge(product_ready, g * KT + k + 1)
                    rows = rows_of(k)
                    last = nc.tensor.matmul(x1_ps[:, :], w0T[0:rows, k, :], products[0:rows, (c * KT + k) % PRING, :],
                                            start=(k == 0), stop=(k == KT - 1))
                    if k == 0 and c > 0:
                        tail_e(it, c - 1)
                    if k == 2 and c > 0:
                        tail_x1T(it, c - 1)
                    if k == 5 and c > 0:
                        tail_g(it, c - 1)
                        if c == 2:
                            transpose_e(it, 1)
                last.then_inc(x1_in_ps, 1)
                if c + 1 < CPI:
                    replicate(it, c + 1, 1)

            def head(it):
                pe.wait_ge(g_ready_act, 2 * CPI * (it + 1))
                pe.wait_ge(g_ready_dve, 2 * CPI * (it + 1))
                for j in range(F):
                    last = nc.tensor.matmul(g_ps[0][:, 0:NB], w1T[:, j, :], G[:, j, :], start=(j == 0), stop=(j == F - 1))
                last.then_inc(z2_in_ps, 1)
                pe.wait_ge(dense_ready, it + 1)
                pe.wait_ge(z2_ready, it + 1)
                for m in range(M1):
                    to = g_ps[1 + m // 2][:, m % 2 * NB:(m % 2 + 1) * NB]
                    mm = slice(m * 128, (m + 1) * 128)
                    nc.tensor.matmul(to, wt1_cin[:, 0, mm], G[:, F, :], start=True, stop=False)
                    nc.tensor.matmul(to, wt1_dense[:, mm], dense_now[:, :], start=False, stop=False)
                    last = nc.tensor.matmul(to, wt1_cin[:, 1, mm], z2[:, :], start=False, stop=True)
                    if m % 2:
                        last.then_inc(h1_in_ps, 1)
                pe.wait_ge(h1_ready, (it + 1) * M1)
                for m in range(M2):
                    for k in range(M1):
                        last = nc.tensor.matmul(g_ps[3][:, m * NB:(m + 1) * NB], wt2[:, k, m * 128:(m + 1) * 128], h1[:, k, :],
                                                start=(k == 0), stop=(k == M1 - 1))
                last.then_inc(h2_in_ps, 1)
                pe.wait_ge(h2_ready, (it + 1) * M2)
                for k in range(M2):
                    last = nc.tensor.matmul(g_ps[0][0:1, 0:NB], wt3[:, k:k + 1], h2[:, k, :], start=(k == 0), stop=(k == M2 - 1))
                last.then_inc(y_in_ps, 1)

            def body(it):
                for c in range(CPI):
                    chunk(it, c)
                tail_e(it, CPI - 1)
                tail_x1T(it, CPI - 1)
                tail_g(it, CPI - 1)
                head(it)

            body(0)
            with pe.Fori(1, ITERS) as it:
                body(it)

        def g_columns(c, r):
            view = G[:, :, c * CB:(c + 1) * CB].rearrange("i f (q r b) -> i r q b f", r=4, b=2)
            return view[:, r, :, :, :]

        def g_bank(r):
            return g_ps[r][:, 0:Q * 2 * FO].rearrange("i (q b f) -> i q b f", b=2, f=FO)

        @block.scalar
        def _(act):
            def copy_eT(it, slot):
                for half in range(2):
                    act.wait_ge(eT_in_ps, it * 2 * TPI + slot * 2 + half + 1)
                    nc.scalar.copy(eT[slot][:, :, half * 8:(half + 1) * 8].rearrange("r b d -> r d b"),
                                   aux_ps[0:ROWS, :].bitcast(bf16).rearrange("r (d b) -> r d b", b=TB)).then_inc(eT_ready, 1)

            def copy_e3(it, c):
                act.wait_ge(e3_in_ps, it * CPI + c + 1)
                nc.scalar.copy(e3[c % 2][:, :], rep_ps[0][0:ROWS, :]).then_inc(e3_ready, 1)

            def copy_x1T(it, c):
                act.wait_ge(x1T_in_ps, it * CPI + c + 1)
                nc.scalar.copy(x1T[:, :, :].rearrange("p q i -> p (q i)"), aux_ps[:, :]).then_inc(x1T_ready, 1)

            def copy_g(it, c):
                act.wait_ge(g_in_ps, it * CPI + c + 1)
                for r in (0, 1):
                    nc.scalar.copy(g_columns(c, r), g_bank(r)).then_inc(g_ready_act, 1)

            def body(it):
                copy_eT(it, 0)
                copy_e3(it, 0)
                after(act, h1_in_ps, it * 2)
                nc.scalar.copy(dense_now[:, :], denseT[:, bass.ds(it * NB, NB)]).then_inc(dense_ready, 1)
                for c in range(CPI):
                    if c > 0:
                        copy_x1T(it, c - 1)
                    if c == 2:
                        copy_g(it, c - 1)
                        copy_eT(it, 1)
                        copy_e3(it, c + 1)
                    else:
                        if c > 0:
                            copy_g(it, c - 1)
                        if c + 1 < CPI:
                            copy_e3(it, c + 1)
                    act.wait_ge(x1_in_ps, it * CPI + c + 1)
                    nc.scalar.copy(x1[:, :], x1_ps[:, :]).then_inc(x1_ready, 1)
                copy_x1T(it, CPI - 1)
                copy_g(it, CPI - 1)
                act.wait_ge(z2_in_ps, it + 1)
                nc.scalar.copy(z2[:, :], g_ps[0][:, 0:NB]).then_inc(z2_ready, 1)
                for m in range(M1):
                    act.wait_ge(h1_in_ps, it * 2 + m // 2 + 1)
                    nc.scalar.activation(h1[:, m, :], g_ps[1 + m // 2][:, m % 2 * NB:(m % 2 + 1) * NB], ACT.Relu,
                                         bias=bias1[:, m:m + 1]).then_inc(h1_ready, 1)
                act.wait_ge(h2_in_ps, it + 1)
                for m in range(M2):
                    nc.scalar.activation(h2[:, m, :], g_ps[3][:, m * NB:(m + 1) * NB], ACT.Relu,
                                         bias=bias2[:, m:m + 1]).then_inc(h2_ready, 1)
                act.wait_ge(y_in_ps, it + 1)
                nc.scalar.copy(y[:, bass.ds(it * NB, NB)], g_ps[0][0:1, 0:NB]).then_inc(y_ready, 1)

            act.wait_ge(mlp_loaded, 6 * 16)
            act.wait_ge(dense_loaded, 16)
            body(0)
            with act.Fori(1, ITERS) as it:
                body(it)

        @block.vector
        def _(dve):
            dve.wait_ge(consts_loaded, 48)
            nc.vector.tensor_copy(ident_b[:, :], ident[:, :]).then_inc(consts_cast, 1)
            nc.vector.tensor_copy(select_b[:, :], select_f[:, :]).then_inc(consts_cast, 1)
            nc.vector.tensor_copy(e_diag[:, :, :, F], mask[:, :].rearrange("p (u b) -> p u b", u=1).to_broadcast([128, Q, 2]))
            dve.wait_ge(w0_loaded, 16)
            nc.vector.tensor_tensor(w0T[:, :, :], w0_both[:, 0, :, :], w0_both[:, 1, :, :], ALU.add).then_inc(w0_summed, 1)
            dve.wait_ge(w0_summed, 1)
            nc.vector.tensor_copy(w0T[0:F, 0, :], w0_both[0:F, 0, 0, :]).then_inc(w0_summed, 1)

            def split(it, slot):
                t = it * TPI + slot
                e = e_rows[slot][:, :].rearrange("b (f d) -> b d f", d=D)
                parts = e_parts[slot]
                dve.wait_ge(gathered[slot], (it + 1) * (16 * F))
                after(dve, eT_in_ps, 2 * (t - 1))
                nc.vector.tensor_copy(parts[:, :, 0, :], e).then_inc(split_step, 1)
                dve.wait_ge(split_step, t * 3 + 1)
                nc.vector.tensor_tensor(e_rest[:, :, :], e, parts[:, :, 0, :], ALU.subtract).then_inc(split_step, 1)
                dve.wait_ge(split_step, t * 3 + 2)
                nc.vector.tensor_copy(parts[:, :, 1, :], e_rest[:, :, :]).then_inc(split_step, 1)
                dve.wait_ge(split_step, t * 3 + 3)
                nc.vector.tensor_tensor(parts[:, :, 2, :], e_rest[:, :, :], parts[:, :, 1, :], ALU.subtract).then_inc(split_done, 1)

            def multiply(it, c, k):
                g = it * CPI + c
                rows = rows_of(k)
                if k == 0:
                    dve.wait_ge(e3_ready, g + 1)
                dve.wait_ge(rep_in_ps, g * KT + k + 1)
                nc.vector.tensor_tensor(products[0:rows, (c * KT + k) % PRING, :], rep_ps[(k + 1) % 2][0:rows, :],
                                        e3[c % 2][0:rows, :], ALU.mult).then_inc(product_ready, 1)

            def diagonal(it, c):
                dve.wait_ge(e_in_ps, it * CPI + c + 1)
                src = aux_ps[:, 0:Q * FO].rearrange("p (q u f) -> p q u f", u=1, f=FO)[:, :, :, 0:F]
                nc.vector.tensor_tensor(e_diag[:, :, :, 0:F], src.to_broadcast([128, Q, 2, F]),
                                        mask[:, :].rearrange("p (u b v) -> p u b v", u=1, v=1).to_broadcast([128, Q, 2, F]),
                                        ALU.mult).then_inc(e_diag_ready, 1)

            def copy_g(it, c):
                dve.wait_ge(g_in_ps, it * CPI + c + 1)
                for r in (2, 3):
                    nc.vector.tensor_copy(g_columns(c, r), g_bank(r)).then_inc(g_ready_dve, 1)

            def body(it):
                split(it, 0)
                for c in range(CPI):
                    for k in range(KT):
                        if k == 2 and c > 1:
                            copy_g(it, c - 2)
                        if k == 3 and c > 0:
                            diagonal(it, c - 1)
                        multiply(it, c, k)
                    if c == 0:
                        split(it, 1)
                copy_g(it, CPI - 2)
                diagonal(it, CPI - 1)
                copy_g(it, CPI - 1)

            body(0)
            with dve.Fori(1, ITERS) as it:
                body(it)


_INS = ["dense_ctx", "ids"] + [f"tbl_{f}" for f in range(F)] + [
    "W_top1", "b_top1", "W_top2", "b_top2", "W_top3", "L0_rec_W0", "L0_rec_W1"]


def _constants():
    select = np.zeros((3, F, ROWS + SHIFTS * F), np.float32)
    for j in range(F):
        for s in range(PER_TILE):
            select[:, j, s * F + j] = 1.0
        for s in range(SHIFTS):
            select[:, (j + s) % F, ROWS + s * F + j] = 1.0
    pair = (np.arange(128)[:, None] // D % 2 == np.arange(2)[None, :]).astype(np.float32)
    return {"select": select.reshape(ROWS, -1), "pair_mask": pair, "identity": np.eye(128, dtype=np.float32)}


def kernel(**inputs):
    import concourse.bacc as _bacc
    from concourse.bass_utils import run_bass_kernel_spmd as _run

    nc = _bacc.Bacc("TRN2", target_bir_lowering=False, num_devices=1)
    arrays, aps = {}, {}
    given = {name: np.ascontiguousarray(inputs[name]) for name in _INS}
    given.update(_constants())
    w0 = given["L0_rec_W0"].reshape(H, F, F)
    j = np.tile(np.arange(F), KT * PER_TILE)
    k = (j + np.repeat(np.arange(KT * PER_TILE), F)) % F
    both = np.stack([w0[:, j, k], w0[:, k, j]])
    given["L0_rec_W0"] = np.ascontiguousarray(both.reshape(2, H, KT, ROWS).transpose(3, 0, 2, 1))
    given["L0_rec_W1"] = np.ascontiguousarray(given["L0_rec_W1"].reshape(H, H, F).transpose(1, 2, 0))
    given["dense_ctx"] = np.ascontiguousarray(given["dense_ctx"].T)
    for name in ("b_top1", "b_top2", "W_top3"):
        given[name] = np.ascontiguousarray(given[name].reshape(-1, 128).T)
    for name, a in given.items():
        arrays[f"in_{name}_dram"] = a
        aps[name] = nc.dram_tensor(f"in_{name}_dram", a.shape, mybir.dt.from_np(a.dtype), kind="ExternalInput").ap()
    out = nc.dram_tensor("out_0_dram", (B, 1), mybir.dt.float32, kind="ExternalOutput").ap()
    cin_tower(nc, aps["dense_ctx"], aps["ids"], [aps[f"tbl_{f}"] for f in range(F)], aps["W_top1"], aps["b_top1"],
              aps["W_top2"], aps["b_top2"], aps["W_top3"], aps["L0_rec_W0"], aps["L0_rec_W1"],
              aps["select"], aps["pair_mask"], aps["identity"], out)
    r = _run(nc, [arrays], core_ids=[0])
    return r.results[0]["out_0_dram"]
```

```python
import numpy as np
import concourse.bass as bass
from concourse import mybir
from contextlib import ExitStack

F = 39
D = 16
B = 2048
H = 128
SHIFTS = (F + 1) // 2
PER_TILE = 3
KT = -(-SHIFTS // PER_TILE)
ROWS = PER_TILE * F
TB = 128
TILES = B // TB
CB = 32
COLS = CB * D
CPT = TB // CB
TPI = 2
CPI = CPT * TPI
NB = TB * TPI
ITERS = B // NB
Q = COLS // 128
QB = CB // Q
FO = F + 1
ET = 4
DPB = D // ET
H1, H2 = 512, 256
M1, M2 = H1 // 128, H2 // 128
RING = 4
GROUPS = 5
PER_GROUP = -(-F // GROUPS)


def after(engine, semaphore, value):
    if isinstance(value, int) and value <= 0:
        return
    engine.wait_ge(semaphore, value)


def rows_of(k):
    return min(PER_TILE, SHIFTS - k * PER_TILE) * F


def group_fields(n):
    return range(n * PER_GROUP, min((n + 1) * PER_GROUP, F))


def chunk_after(it, c):
    return (it, c + 1) if c + 1 < CPI else (it + 1, 0)


def chunk_before(it, c):
    return (it, c - 1) if c else (it - 1, CPI - 1)


def cin_tower(nc, dense_t, ids, tables, w_top1, b_top1, w_top2, b_top2, w_top3, w0, w1,
              select, identity, out):
    f32, f32r, i32 = mybir.dt.float32, mybir.dt.float32r, mybir.dt.int32
    ALU = mybir.AluOpType
    ACT = mybir.ActivationFunctionType
    ctx = ExitStack()
    with ctx:
        def sb(name, shape, dt=f32):
            return ctx.enter_context(nc.sbuf_tensor(name, shape, dt))

        def ps(name, shape, dt=f32):
            return ctx.enter_context(nc.psum_tensor(name, shape, dt))

        def sem(name):
            return ctx.enter_context(nc.semaphore(name))

        SELECTED = ROWS + SHIFTS * F + 2 * FO
        select_r = sb("select_r", [2 * F, SELECTED], f32r)
        ident = sb("ident", [128, 128])
        w0_hi = sb("w0_hi", [ROWS, KT, H], f32r)
        w0_lo = sb("w0_lo", [ROWS, KT, H], f32r)
        w1T = sb("w1T", [H, F, H])
        wt1_cin = sb("wt1_cin", [128, 2, H1])
        wt1_dense = sb("wt1_dense", [D, H1])
        wt2 = sb("wt2", [128, M1, H2])
        wt3 = sb("wt3", [128, M2])
        bias1 = sb("bias1", [128, M1])
        bias2 = sb("bias2", [128, M2])
        ids_sb = [sb(f"ids_sb{n}", [128, F], i32) for n in range(2)]
        e_rows = [sb(f"e_rows{n}", [128, F * D]) for n in range(2)]
        e_parts = sb("e_parts", [128, D, 2, F])
        eT = [sb(f"eT{n}", [2 * F, TB, D], f32r) for n in range(2)]
        e3 = [sb(f"e3_{n}", [ROWS, COLS]) for n in range(2)]
        products = sb("products", [ROWS, RING, COLS])
        product_hi = sb("product_hi", [ROWS, RING, COLS], f32r)
        product_lo = sb("product_lo", [ROWS, RING, COLS], f32r)
        x1 = sb("x1", [H, COLS])
        x1T_hi = sb("x1T_hi", [128, Q, H], f32r)
        x1T_lo = sb("x1T_lo", [128, Q, H], f32r)
        e_cols = sb("e_cols", [128, Q, 2, FO], f32r)
        e_diag = sb("e_diag", [128, QB, Q, 2, FO], f32r)
        G = sb("G", [H, FO, 2 * NB])
        staging = G[:, :, :].rearrange("p f b -> p (f b)")
        w0_both = staging[0:ROWS, 0:2 * KT * H].rearrange("p (a k h) -> p a k h", a=2, k=KT)
        w0_sum = w0_both[:, 0, :, :]
        select_f = staging[0:2 * F, 2 * KT * H:2 * KT * H + SELECTED]
        z2 = sb("z2", [H, NB])
        dense_now = sb("dense_now", [D, NB])
        h1 = sb("h1", [128, M1, NB])
        h2 = sb("h2", [128, M2, NB])
        y = sb("y", [1, NB])

        rep_ps = [ps(f"rep_ps{n}", [128, COLS]) for n in range(2)]
        x1_ps = ps("x1_ps", [H, COLS])
        aux_ps = ps("aux_ps", [128, 512])
        g_ps = [ps(f"g_ps{n}", [128, 512]) for n in range(Q)]

        consts_loaded = sem("consts_loaded")
        w0_loaded = sem("w0_loaded")
        w1_loaded = sem("w1_loaded")
        dense_loaded = sem("dense_loaded")
        mlp_loaded = sem("mlp_loaded")
        select_ready = sem("select_ready")
        diag_initialised = sem("diag_initialised")
        w0_step = sem("w0_step")
        w0_split = sem("w0_split")
        ids_loaded = [sem(f"ids_loaded{n}") for n in range(2)]
        gathered = [sem(f"gathered{n}") for n in range(2)]
        tiles_begun = sem("tiles_begun")
        e_hi_ready = sem("e_hi_ready")
        split_done = sem("split_done")
        eT_in_ps = sem("eT_in_ps")
        eT_ready = sem("eT_ready")
        e3_in_ps = sem("e3_in_ps")
        e3_ready = sem("e3_ready")
        rep_in_ps = sem("rep_in_ps")
        product_ready = sem("product_ready")
        hi_ready = sem("hi_ready")
        lo_ready = sem("lo_ready")
        x1_in_ps = sem("x1_in_ps")
        x1_ready = sem("x1_ready")
        e_in_ps = sem("e_in_ps")
        e_cols_ready = sem("e_cols_ready")
        e_diag_ready = sem("e_diag_ready")
        x1T_in_ps = sem("x1T_in_ps")
        x1T_hi_ready = sem("x1T_hi_ready")
        x1T_lo_ready = sem("x1T_lo_ready")
        g_in_ps = sem("g_in_ps")
        g_ready = sem("g_ready")
        z2_in_ps = sem("z2_in_ps")
        z2_ready = sem("z2_ready")
        h1_in_ps = sem("h1_in_ps")
        h1_ready = sem("h1_ready")
        h2_in_ps = sem("h2_in_ps")
        h2_ready = sem("h2_ready")
        y_in_ps = sem("y_in_ps")
        y_ready = sem("y_ready")
        y_stored = sem("y_stored")

        block = ctx.enter_context(nc.Block())

        @block.sync
        def _(sp):
            for slot in range(TPI):
                sp.dma_start(ids_sb[slot][:, :], ids[slot * TB:(slot + 1) * TB, :]).then_inc(ids_loaded[slot], 16)
            sp.dma_start(ident[:, :], identity).then_inc(consts_loaded, 16)
            sp.dma_start(select_f, select).then_inc(consts_loaded, 16)
            sp.dma_start(w0_both, w0).then_inc(w0_loaded, 16)
            sp.dma_start(w1T[:, :, :], w1).then_inc(w1_loaded, 16)
            sp.dma_start(wt1_cin[:, :, :], w_top1[0:2 * H, :].rearrange("(k p) n -> p k n", p=128)).then_inc(mlp_loaded, 16)
            sp.dma_start(wt1_dense[:, :], w_top1[2 * H:2 * H + D, :]).then_inc(mlp_loaded, 16)
            sp.dma_start(wt2[:, :, :], w_top2.rearrange("(k p) n -> p k n", p=128)).then_inc(mlp_loaded, 16)
            sp.dma_start(wt3[:, :], w_top3).then_inc(mlp_loaded, 16)
            sp.dma_start(bias1[:, :], b_top1).then_inc(mlp_loaded, 16)
            sp.dma_start(bias2[:, :], b_top2).then_inc(mlp_loaded, 16)

            def spread(it, c):
                g = it * CPI + c
                sp.wait_ge(e_cols_ready, g + 1)
                after(sp, g_in_ps, g)
                for b in range(QB):
                    sp.dma_start(e_diag[b * D:(b + 1) * D, b, :, :, :].rearrange("p q a f -> p (q a f)").bitcast(f32),
                                 e_cols[b * D:(b + 1) * D, :, :, :].rearrange("p q a f -> p (q a f)").bitcast(f32)).then_inc(e_diag_ready, 16)

            def load_dense(it):
                after(sp, h1_in_ps, 2 * it)
                sp.dma_start(dense_now[:, :], dense_t[:, bass.ds(it * NB, NB)]).then_inc(dense_loaded, 16)

            def body(it, first=False, final=False):
                for c in range(CPI):
                    spread(it, c)
                    if c == 2 and not first:
                        load_dense(it - 1)
                    if c % CPT == 0 and not final:
                        slot = c // CPT
                        sp.wait_ge(gathered[slot], (it + 1) * (16 * F))
                        sp.dma_start(ids_sb[slot][:, :], ids[bass.ds((it + 1) * NB + slot * TB, TB), :]).then_inc(ids_loaded[slot], 16)

            sp.wait_ge(diag_initialised, 1)
            body(0, first=True)
            with sp.Fori(1, ITERS - 1) as it:
                body(it)
            body(ITERS - 1, final=True)
            load_dense(ITERS - 1)
            sp.wait_ge(y_stored, 16 * ITERS)

        @block.gpsimd
        def _(pool):
            def body(it):
                for slot in range(TPI):
                    pool.wait_ge(ids_loaded[slot], it * 16 + 16)
                    after(pool, split_done, (it - 1) * TPI + slot + 1)
                    pool.sem_inc(tiles_begun, 1)
                    for f in range(F):
                        nc.gpsimd.indirect_dma_start(
                            out=e_rows[slot][:, f * D:(f + 1) * D], out_offset=None, in_=tables[f],
                            in_offset=bass.IndirectOffsetOnAxis(ap=ids_sb[slot][:, f:f + 1], axis=0),
                        ).then_inc(gathered[slot], 16)

            body(0)
            with pool.Fori(1, ITERS) as it:
                body(it)

        @block.tensor
        def _(pe):
            def columns(c):
                return eT[c // CPT][:, :, :].rearrange("r b d -> r (b d)")[:, c % CPT * COLS:(c % CPT + 1) * COLS]

            def transpose_e(t, batches, banks):
                pe.wait_ge(split_done, t + 1)
                for n, bank in zip(batches, banks):
                    if n > bank:
                        pe.wait_ge(eT_ready, t * ET + 1)
                    for m in range(DPB):
                        last = nc.tensor.transpose(g_ps[bank][0:2 * F, m * TB:(m + 1) * TB],
                                                   e_parts[:, n * DPB + m, :, :].rearrange("b q f -> b (q f)"), ident[:, :])
                    last.then_inc(eT_in_ps, 1)

            def replicate_e3(it, c):
                g = it * CPI + c
                if c % CPT == 0:
                    pe.wait_ge(eT_ready, (it * TPI + c // CPT + 1) * ET)
                after(pe, product_ready, g * KT - 1)
                nc.tensor.matmul(rep_ps[0][0:ROWS, :], select_r[:, 0:ROWS], columns(c), start=True, stop=True).then_inc(e3_in_ps, 1)

            def replicate(it, c, k):
                g = it * CPI + c
                if k == 1:
                    pe.wait_ge(e3_ready, g + 1)
                else:
                    after(pe, product_ready, g * KT + max(k - 1, 0))
                rows = rows_of(k)
                nc.tensor.matmul(rep_ps[(k + 1) % 2][0:rows, :], select_r[:, ROWS + k * ROWS:ROWS + k * ROWS + rows],
                                 columns(c), start=True, stop=True).then_inc(rep_in_ps, 1)

            def contract(it, c, k):
                g = it * CPI + c
                if k == 0:
                    after(pe, x1_ready, g)
                pe.wait_ge(hi_ready, g * KT + k + 1)
                rows, slot = rows_of(k), (c * KT + k) % RING
                nc.tensor.matmul(x1_ps[:, :], w0_hi[0:rows, k, :], product_hi[0:rows, slot, :], start=(k == 0), stop=False)
                nc.tensor.matmul(x1_ps[:, :], w0_lo[0:rows, k, :], product_hi[0:rows, slot, :], start=False, stop=False)
                pe.wait_ge(lo_ready, g * KT + k + 1)
                last = nc.tensor.matmul(x1_ps[:, :], w0_hi[0:rows, k, :], product_lo[0:rows, slot, :],
                                        start=False, stop=(k == KT - 1))
                if k == KT - 1:
                    last.then_inc(x1_in_ps, 1)

            def spread_e(it, c):
                after(pe, x1T_lo_ready, it * CPI + c)
                for q in range(Q):
                    last = nc.tensor.matmul(aux_ps[:, q * 2 * FO:(q + 1) * 2 * FO], columns(c)[:, q * 128:(q + 1) * 128],
                                            select_r[:, ROWS + SHIFTS * F:SELECTED], start=True, stop=True)
                last.then_inc(e_in_ps, 1)

            def transpose_x1(it, c):
                g = it * CPI + c
                pe.wait_ge(x1_ready, g + 1)
                pe.wait_ge(e_cols_ready, g + 1)
                for q in range(Q):
                    last = nc.tensor.transpose(aux_ps[:, q * 128:(q + 1) * 128], x1[:, q * 128:(q + 1) * 128], ident[:, :])
                last.then_inc(x1T_in_ps, 1)

            def make_g(it, c):
                g = it * CPI + c
                pe.wait_ge(x1T_hi_ready, g + 1)
                pe.wait_ge(x1T_lo_ready, g + 1)
                pe.wait_ge(e_diag_ready, (g + 1) * (16 * QB))
                after(pe, g_ready, Q * g)
                for q in range(Q):
                    for n, (x, part) in enumerate(((x1T_hi, 0), (x1T_hi, 1), (x1T_lo, 0))):
                        last = nc.tensor.matmul(g_ps[q][:, 0:QB * FO], x[:, q, :], e_diag[:, :, q, part, :],
                                                start=(n == 0), stop=(n == 2))
                last.then_inc(g_in_ps, 1)

            def layer1(it, fields, n, bank):
                for j in fields:
                    last = nc.tensor.matmul(g_ps[bank][:, 0:NB], w1T[:, j, :], G[:, j, bass.ds(it % 2 * NB, NB)],
                                            start=(j == group_fields(n)[0]), stop=(j == group_fields(n)[-1]))
                if fields[-1] == group_fields(n)[-1]:
                    last.then_inc(z2_in_ps, 1)

            def mlp1(it, pair):
                pe.wait_ge(dense_loaded, 16 * (it + 1))
                pe.wait_ge(z2_ready, (it + 1) * GROUPS)
                for n in range(2):
                    m = 2 * pair + n
                    to = g_ps[1 + pair][:, n * NB:(n + 1) * NB]
                    mm = slice(m * 128, (m + 1) * 128)
                    nc.tensor.matmul(to, wt1_cin[:, 0, mm], G[:, F, bass.ds(it % 2 * NB, NB)], start=True, stop=False)
                    nc.tensor.matmul(to, wt1_dense[:, mm], dense_now[:, :], start=False, stop=False)
                    last = nc.tensor.matmul(to, wt1_cin[:, 1, mm], z2[:, :], start=False, stop=True)
                last.then_inc(h1_in_ps, 1)

            def mlp2(it, m):
                pe.wait_ge(h1_ready, (it + 1) * M1)
                for k in range(M1):
                    last = nc.tensor.matmul(g_ps[0][:, m * NB:(m + 1) * NB], wt2[:, k, m * 128:(m + 1) * 128], h1[:, k, :],
                                            start=(k == 0), stop=(k == M1 - 1))
                if m == M2 - 1:
                    last.then_inc(h2_in_ps, 1)

            def mlp3(it):
                pe.wait_ge(h2_ready, (it + 1) * M2)
                for k in range(M2):
                    last = nc.tensor.matmul(g_ps[0][0:1, 0:NB], wt3[:, k:k + 1], h2[:, k, :], start=(k == 0), stop=(k == M2 - 1))
                last.then_inc(y_in_ps, 1)

            def chunk(it, c, first=False, final=False):
                g = it * CPI + c
                has_last = not (first and c == 0)
                has_next = not (final and c == CPI - 1)
                makes_eT = c % CPT == CPT - 1 and has_next
                for k in range(KT):
                    for ahead in ((2, 3) if k == 0 else (k + 3,)):
                        if ahead < KT:
                            replicate(it, c, ahead)
                        elif has_next and ahead == KT:
                            replicate_e3(*chunk_after(it, c))
                        elif has_next:
                            replicate(*chunk_after(it, c), ahead - KT - 1)
                    contract(it, c, k)
                    if k == 0 and has_last:
                        spread_e(*chunk_before(it, c))
                    if k == 1 and makes_eT:
                        after(pe, g_ready, Q * (g - 1))
                        transpose_e(it * TPI + c // CPT + 1, (0, 1), (1, 2))
                    if k == 2 and has_last:
                        transpose_x1(*chunk_before(it, c))
                    if k == 2 and makes_eT:
                        transpose_e(it * TPI + c // CPT + 1, (2, 3), (3, 1))
                    if not first:
                        if 1 <= c <= GROUPS and 2 <= k <= 4:
                            pe.wait_ge(g_ready, Q * (g - 1))
                            fields = group_fields(c - 1)[3 * (k - 2):3 * (k - 1)]
                            layer1(it - 1, fields, c - 1, 0)
                        if c == 6 and 2 <= k <= 3:
                            pe.wait_ge(g_ready, Q * (g - 1))
                            mlp1(it - 1, k - 2)
                        if c == 7 and 2 <= k <= 3:
                            pe.wait_ge(g_ready, Q * (g - 1))
                            mlp2(it - 1, k - 2)
                        if c == 7 and k == 5:
                            mlp3(it - 1)
                if has_last:
                    if not first:
                        if 1 <= c <= GROUPS:
                            pe.wait_ge(z2_ready, (it - 1) * GROUPS + c)
                        if c == 6:
                            pe.wait_ge(h1_ready, it * M1)
                        if c == 7:
                            pe.wait_ge(y_ready, it)
                    if makes_eT:
                        pe.wait_ge(eT_ready, (it * TPI + c // CPT + 2) * ET)
                    make_g(*chunk_before(it, c))

            pe.wait_ge(consts_loaded, 32)
            transpose_e(0, (0, 1, 2, 3), (0, 1, 2, 3))
            pe.wait_ge(select_ready, 1)
            pe.wait_ge(w0_split, 2)
            replicate_e3(0, 0)
            replicate(0, 0, 0)
            replicate(0, 0, 1)
            for c in range(CPI):
                chunk(0, c, first=True)
            pe.wait_ge(w1_loaded, 16)
            pe.wait_ge(mlp_loaded, 6 * 16)
            with pe.Fori(1, ITERS - 1) as it:
                for c in range(CPI):
                    chunk(it, c)
            end = ITERS - 1
            for c in range(CPI):
                chunk(end, c, final=True)
            spread_e(end, CPI - 1)
            transpose_x1(end, CPI - 1)
            make_g(end, CPI - 1)
            pe.wait_ge(g_ready, Q * CPI * ITERS)
            for n in range(GROUPS):
                if n >= Q:
                    pe.wait_ge(z2_ready, end * GROUPS + n - Q + 1)
                layer1(end, group_fields(n), n, n % Q)
            for pair in range(M1 // 2):
                mlp1(end, pair)
            for m in range(M2):
                mlp2(end, m)
            mlp3(end)

        @block.scalar
        def _(act):
            def copy_eT(slot, t, batches, banks):
                for n, bank in zip(batches, banks):
                    act.wait_ge(eT_in_ps, t * ET + n + 1)
                    nc.scalar.copy(eT[slot][:, :, n * DPB:(n + 1) * DPB].rearrange("r b d -> r d b"),
                                   g_ps[bank][0:2 * F, :].rearrange("r (d b) -> r d b", b=TB)).then_inc(eT_ready, 1)

            def copy_e3(it, c):
                act.wait_ge(e3_in_ps, it * CPI + c + 1)
                nc.scalar.copy(e3[c % 2][:, :], rep_ps[0][0:ROWS, :]).then_inc(e3_ready, 1)

            def round_product(it, c, k):
                g = it * CPI + c
                act.wait_ge(product_ready, g * KT + k + 1)
                n, rows = c * KT + k, rows_of(k)
                nc.scalar.copy(product_hi[0:rows, n % RING, :], products[0:rows, n % RING, :]).then_inc(hi_ready, 1)

            def copy_x1(it, c):
                act.wait_ge(x1_in_ps, it * CPI + c + 1)
                nc.scalar.copy(x1[:, :], x1_ps[:, :]).then_inc(x1_ready, 1)

            def round_x1T(it, c):
                act.wait_ge(x1T_in_ps, it * CPI + c + 1)
                nc.scalar.copy(x1T_hi[:, :, :].rearrange("p q i -> p (q i)"), aux_ps[:, :]).then_inc(x1T_hi_ready, 1)

            def copy_g(it, c, banks):
                act.wait_ge(g_in_ps, it * CPI + c + 1)
                for q in banks:
                    nc.scalar.copy(G[:, :, bass.ds(it % 2 * NB + c * CB + q * QB, QB)].rearrange("i f b -> i b f"),
                                   g_ps[q][:, 0:QB * FO].rearrange("i (b f) -> i b f", f=FO)).then_inc(g_ready, 1)

            def relu1(it, pair):
                act.wait_ge(h1_in_ps, it * 2 + pair + 1)
                for m in (2 * pair, 2 * pair + 1):
                    nc.scalar.activation(h1[:, m, :], g_ps[1 + pair][:, m % 2 * NB:(m % 2 + 1) * NB], ACT.Relu,
                                         bias=bias1[:, m:m + 1]).then_inc(h1_ready, 1)

            def relu2(it):
                act.wait_ge(h2_in_ps, it + 1)
                for m in range(M2):
                    nc.scalar.activation(h2[:, m, :], g_ps[0][:, m * NB:(m + 1) * NB], ACT.Relu,
                                         bias=bias2[:, m:m + 1]).then_inc(h2_ready, 1)

            def store_y(it):
                act.wait_ge(y_in_ps, it + 1)
                after(act, y_stored, 16 * it)
                nc.scalar.copy(y[:, :], g_ps[0][0:1, 0:NB]).then_inc(y_ready, 1)
                act.wait_ge(y_ready, it + 1)
                act.dma_start(out.rearrange("b o -> o b")[:, bass.ds(it * NB, NB)], y[:, :]).then_inc(y_stored, 16)

            def chunk(it, c, first=False, final=False):
                has_last = not (first and c == 0)
                has_last2 = not (first and c <= 1)
                has_next = not (final and c == CPI - 1)
                makes_eT = c % CPT == CPT - 1 and has_next
                last = chunk_before(it, c)
                next_slot, next_tile = (c // CPT + 1) % TPI, it * TPI + c // CPT + 1
                if has_last:
                    copy_x1(*last)
                for k in range(KT):
                    if k == 4 and has_next:
                        copy_e3(*chunk_after(it, c))
                    if k + 1 < KT:
                        round_product(it, c, k + 1)
                    elif has_next:
                        round_product(*chunk_after(it, c), 0)
                    if k == 0 and has_last2:
                        copy_g(*chunk_before(*last), (0, 1))
                    if k == 1 and has_last2:
                        copy_g(*chunk_before(*last), (2, 3))
                    if k == 1 and makes_eT:
                        copy_eT(next_slot, next_tile, (0, 1), (1, 2))
                    if k == 2 and makes_eT:
                        copy_eT(next_slot, next_tile, (2, 3), (3, 1))
                    if k == 2 and has_last:
                        round_x1T(*last)
                    if not first:
                        if c == 6 and 3 <= k <= 4:
                            relu1(it - 1, k - 3)
                        if c == 7 and k == 4:
                            relu2(it - 1)
                        if c == 7 and k == 5:
                            store_y(it - 1)

            copy_eT(0, 0, (0, 1, 2, 3), (0, 1, 2, 3))
            act.wait_ge(mlp_loaded, 6 * 16)
            copy_e3(0, 0)
            round_product(0, 0, 0)
            for c in range(CPI):
                chunk(0, c, first=True)
            with act.Fori(1, ITERS - 1) as it:
                for c in range(CPI):
                    chunk(it, c)
            end = ITERS - 1
            for c in range(CPI):
                chunk(end, c, final=True)
            copy_x1(end, CPI - 1)
            copy_g(end, CPI - 2, (0, 1, 2, 3))
            round_x1T(end, CPI - 1)
            copy_g(end, CPI - 1, (0, 1, 2, 3))
            for pair in range(M1 // 2):
                relu1(end, pair)
            relu2(end)
            store_y(end)

        @block.vector
        def _(dve):
            dve.wait_ge(consts_loaded, 32)
            nc.vector.tensor_copy(select_r[:, :], select_f).then_inc(select_ready, 1)
            nc.vector.memset(e_diag[:, :, :, :, :].bitcast(f32), 0.0).then_inc(diag_initialised, 1)
            nc.vector.memset(e_cols[:, :, 0, F].bitcast(f32), 1.0)
            nc.vector.memset(e_cols[:, :, 1, F].bitcast(f32), 0.0)
            dve.wait_ge(w0_loaded, 16)
            nc.vector.memset(w0_both[0:F, 1, 0, :], 0.0).then_inc(w0_step, 1)
            dve.wait_ge(w0_step, 1)
            nc.vector.tensor_tensor(w0_sum, w0_sum, w0_both[:, 1, :, :], ALU.add).then_inc(w0_step, 1)
            dve.wait_ge(w0_step, 2)
            nc.vector.tensor_copy(w0_hi[:, :, :], w0_sum).then_inc(w0_split, 1)
            dve.wait_ge(w0_split, 1)
            nc.vector.tensor_tensor(w0_lo[:, :, :], w0_sum, w0_hi[:, :, :].bitcast(f32), ALU.subtract).then_inc(w0_split, 1)

            def split(t, it, slot):
                e = e_rows[slot][:, :].rearrange("b (f d) -> b d f", d=D)
                dve.wait_ge(gathered[slot], (it + 1) * (16 * F))
                after(dve, eT_in_ps, ET * t)
                nc.vector.tensor_copy(e_parts[:, :, 0, :].bitcast(f32r), e).then_inc(e_hi_ready, 1)
                dve.wait_ge(e_hi_ready, t + 1)
                nc.vector.tensor_tensor(e_parts[:, :, 1, :], e, e_parts[:, :, 0, :], ALU.subtract).then_inc(split_done, 1)

            def multiply(it, c, k):
                g = it * CPI + c
                n, rows = c * KT + k, rows_of(k)
                if k == 0:
                    dve.wait_ge(e3_ready, g + 1)
                dve.wait_ge(rep_in_ps, g * KT + k + 1)
                nc.vector.tensor_tensor(products[0:rows, n % RING, :], rep_ps[(k + 1) % 2][0:rows, :],
                                        e3[c % 2][0:rows, :], ALU.mult).then_inc(product_ready, 1)

            def lower_part(it, c, k):
                g = it * CPI + c
                n, rows = c * KT + k, rows_of(k)
                dve.wait_ge(hi_ready, g * KT + k + 1)
                nc.vector.tensor_tensor(product_lo[0:rows, n % RING, :], products[0:rows, n % RING, :],
                                        product_hi[0:rows, n % RING, :].bitcast(f32), ALU.subtract).then_inc(lo_ready, 1)

            def copy_e(it, c):
                g = it * CPI + c
                dve.wait_ge(e_in_ps, g + 1)
                after(dve, e_diag_ready, g * (16 * QB))
                nc.vector.tensor_copy(e_cols[:, :, :, 0:F], aux_ps[:, 0:Q * 2 * FO].rearrange("p (q a f) -> p q a f", a=2, f=FO)[:, :, :, 0:F]).then_inc(e_cols_ready, 1)

            def lower_x1T(it, c):
                dve.wait_ge(x1T_hi_ready, it * CPI + c + 1)
                nc.vector.tensor_tensor(x1T_lo[:, :, :].rearrange("p q i -> p (q i)"), aux_ps[:, :],
                                        x1T_hi[:, :, :].rearrange("p q i -> p (q i)").bitcast(f32),
                                        ALU.subtract).then_inc(x1T_lo_ready, 1)

            def add_layer1(it, n, bank):
                dve.wait_ge(z2_in_ps, it * GROUPS + n + 1)
                if n == 0:
                    nc.vector.tensor_copy(z2[:, :], g_ps[bank][:, 0:NB]).then_inc(z2_ready, 1)
                else:
                    dve.wait_ge(z2_ready, it * GROUPS + n)
                    nc.vector.tensor_tensor(z2[:, :], g_ps[bank][:, 0:NB], z2[:, :], ALU.add).then_inc(z2_ready, 1)

            def chunk(it, c, first=False, final=False):
                has_last = not (first and c == 0)
                has_next = not (final and c == CPI - 1)
                last = chunk_before(it, c)
                for k in range(KT):
                    if k + 1 < KT:
                        multiply(it, c, k + 1)
                    elif has_next:
                        multiply(*chunk_after(it, c), 0)
                    lower_part(it, c, k)
                    if k == 1 and has_last:
                        copy_e(*last)
                    if k == 3 and has_last:
                        lower_x1T(*last)
                    if k == 4 and c == 2:
                        split(it * TPI + 1, it, 1)
                    if k == 4 and c == 6 and not final:
                        split(it * TPI + 2, it + 1, 0)
                    if k == 4 and 1 <= c <= GROUPS and not first:
                        add_layer1(it - 1, c - 1, 0)

            split(0, 0, 0)
            multiply(0, 0, 0)
            for c in range(CPI):
                chunk(0, c, first=True)
            with dve.Fori(1, ITERS - 1) as it:
                for c in range(CPI):
                    chunk(it, c)
            end = ITERS - 1
            for c in range(CPI):
                chunk(end, c, final=True)
            copy_e(end, CPI - 1)
            lower_x1T(end, CPI - 1)
            for n in range(GROUPS):
                add_layer1(end, n, n % Q)


_INS = ["dense_ctx", "ids"] + [f"tbl_{f}" for f in range(F)] + [
    "W_top1", "b_top1", "W_top2", "b_top2", "W_top3", "L0_rec_W0", "L0_rec_W1"]


def _constants():
    copies = np.zeros((2, F, ROWS + SHIFTS * F), np.float32)
    for j in range(F):
        for s in range(PER_TILE):
            copies[:, j, s * F + j] = 1.0
        for s in range(SHIFTS):
            copies[:, (j + s) % F, ROWS + s * F + j] = 1.0
    parts = np.zeros((2, F, 2, FO), np.float32)
    for part in range(2):
        parts[part, np.arange(F), part, np.arange(F)] = 1.0
    select = np.concatenate([copies.reshape(2 * F, -1), parts.reshape(2 * F, -1)], axis=1)
    return {"select": select, "identity": np.eye(128, dtype=np.float32)}


def kernel(**inputs):
    import concourse.bacc as _bacc
    from concourse.bass_utils import run_bass_kernel_spmd as _run

    nc = _bacc.Bacc("TRN2", target_bir_lowering=False, num_devices=1)
    arrays, aps = {}, {}
    given = {name: np.ascontiguousarray(inputs[name]) for name in _INS}
    given.update(_constants())
    w0 = given["L0_rec_W0"].reshape(H, F, F)
    j = np.tile(np.arange(F), KT * PER_TILE)
    k = (j + np.repeat(np.arange(KT * PER_TILE), F)) % F
    both = np.stack([w0[:, j, k], w0[:, k, j]])
    given["L0_rec_W0"] = np.ascontiguousarray(both.reshape(2, H, KT, ROWS).transpose(3, 0, 2, 1))
    given["L0_rec_W1"] = np.ascontiguousarray(given["L0_rec_W1"].reshape(H, H, F).transpose(1, 2, 0))
    given["dense_ctx"] = np.ascontiguousarray(given["dense_ctx"].T)
    for name in ("b_top1", "b_top2", "W_top3"):
        given[name] = np.ascontiguousarray(given[name].reshape(-1, 128).T)
    for name, a in given.items():
        arrays[f"in_{name}_dram"] = a
        aps[name] = nc.dram_tensor(f"in_{name}_dram", a.shape, mybir.dt.from_np(a.dtype), kind="ExternalInput").ap()
    out = nc.dram_tensor("out_0_dram", (B, 1), mybir.dt.float32, kind="ExternalOutput").ap()
    cin_tower(nc, aps["dense_ctx"], aps["ids"], [aps[f"tbl_{f}"] for f in range(F)], aps["W_top1"], aps["b_top1"],
              aps["W_top2"], aps["b_top2"], aps["W_top3"], aps["L0_rec_W0"], aps["L0_rec_W1"],
              aps["select"], aps["identity"], out)
    r = _run(nc, [arrays], core_ids=[0])
    return r.results[0]["out_0_dram"]
```

```python
import numpy as np
import concourse.bass as bass
from concourse import mybir
from contextlib import ExitStack

F = 39
D = 16
B = 2048
H = 128
SHIFTS = (F + 1) // 2
PER_TILE = 3
KT = -(-SHIFTS // PER_TILE)
ROWS = PER_TILE * F
TB = 128
TILES = B // TB
CB = 32
COLS = CB * D
CPT = TB // CB
TPI = 2
CPI = CPT * TPI
NB = TB * TPI
ITERS = B // NB
Q = COLS // 128
QB = CB // Q
FO = F + 1
ET = 4
DPB = D // ET
H1, H2 = 512, 256
M1, M2 = H1 // 128, H2 // 128
ET_STEPS = ((2, 4), (2, 5), (2, 6), (3, 0))
MLP1_STEPS = ((6, 5), (6, 6), (7, 0), (7, 2), (7, 3), (7, 4))
MLP2_STEPS = ((0, 1), (0, 2), (0, 3), (0, 4))
MLP3_STEP = (0, 6)
DENSE_STEP = (4, 2)
LO_RING = 2
RING = 3
BY_DMA = 3
BY_PE = KT - BY_DMA
REPS = BY_PE
CYCLE = ROWS + KT
REP_BANKS = 2
GAP = 32
ITEMS_AT = ((3,), (4,), (5,), (), (6,), (), ())
LAYER1 = ((0, 2, 1, 1, 1, 1, 1), (1, 1, 1, 1, 0, 0, 0), *3 * ((2, 1, 1, 1, 1, 1, 1),), (1, 1, 1, 1, 0, 0, 0))


def after(engine, semaphore, value):
    if isinstance(value, int) and value <= 0:
        return
    engine.wait_ge(semaphore, value)


def held_in_slot(c, k):
    return 2 if c == 0 and k < 2 else RING


def rows_of(k):
    return sum(k + n * KT < SHIFTS for n in range(PER_TILE)) * F


def fields_at(c, k):
    if not 1 <= c <= len(LAYER1):
        return range(0)
    first = sum(map(sum, LAYER1[:c - 1])) + sum(LAYER1[c - 1][:k])
    return range(first, first + LAYER1[c - 1][k])


def rep_bank(c, item):
    return (c * REPS + item) % REP_BANKS


def rep_before(c, item):
    bank, back = rep_bank(c, item), 0
    while True:
        item -= 1
        if item < 0:
            item, c, back = REPS - 1, (c - 1) % CPI, back + 1
        if rep_bank(c, item) == bank:
            return back, item


def chunk_after(it, c):
    return (it, c + 1) if c + 1 < CPI else (it + 1, 0)


def chunk_before(it, c):
    return (it, c - 1) if c else (it - 1, CPI - 1)


def cin_tower(nc, dense_t, ids, tables, w_top1, b_top1, w_top2, b_top2, w_top3, w0, w1,
              select, identity, e_scratch, out):
    f32, f32r, i32 = mybir.dt.float32, mybir.dt.float32r, mybir.dt.int32
    ALU = mybir.AluOpType
    ACT = mybir.ActivationFunctionType
    ctx = ExitStack()
    with ctx:
        def sb(name, shape, dt=f32):
            return ctx.enter_context(nc.sbuf_tensor(name, shape, dt))

        def ps(name, shape, dt=f32):
            return ctx.enter_context(nc.psum_tensor(name, shape, dt))

        def sem(name):
            return ctx.enter_context(nc.semaphore(name))

        SELECTED = CYCLE
        select_r = sb("select_r", [2 * FO, SELECTED], f32r)
        ident = sb("ident", [128, 128])
        w0_hi = sb("w0_hi", [ROWS, KT, H], f32r)
        w0_lo = sb("w0_lo", [ROWS, KT, H], f32r)
        w1T = sb("w1T", [H, F, H])
        wt1_cin = sb("wt1_cin", [128, 2, H1])
        wt1_dense = sb("wt1_dense", [3 * GAP, H1], f32r)
        wt2 = sb("wt2", [128, M1, H2])
        wt3 = sb("wt3", [128, M2])
        bias1 = sb("bias1", [128, M1])
        bias2 = sb("bias2", [128, M2])
        ids_sb = [sb(f"ids_sb{n}", [128, F], i32) for n in range(2)]
        e_rows = [sb(f"e_rows{n}", [128, F * D]) for n in range(2)]
        e_parts = sb("e_parts", [128, D, 2, FO])
        eT = [sb(f"eT{n}", [2 * FO, TB, D], f32r) for n in range(2)]
        cycle = [sb(f"cycle{n}", [CYCLE, COLS]) for n in range(2)]
        left = [sb(f"left{n}", [ROWS, COLS]) for n in range(2)]
        shifted = sb("shifted", [ROWS, BY_DMA, COLS])
        products = sb("products", [ROWS, RING, COLS])
        product_hi = sb("product_hi", [ROWS, RING, COLS], f32r)
        product_lo = sb("product_lo", [ROWS, LO_RING, COLS], f32r)
        x1 = sb("x1", [H, COLS])
        x1T_hi = sb("x1T_hi", [128, Q, H], f32r)
        x1T_lo = sb("x1T_lo", [128, Q, H], f32r)
        e_diag = [sb(f"e_diag{n}", [128, QB, Q, 2, FO], f32r) for n in range(2)]
        G = sb("G", [H, FO, 2 * NB])
        staging = G[:, :, :].rearrange("p f b -> p (f b)")
        w0_both = staging[0:ROWS, 0:2 * KT * H].rearrange("p (a k h) -> p a k h", a=2, k=KT)
        w0_sum = w0_both[:, 0, :, :]
        wt1_dense_f = staging[0:3 * GAP, 2 * KT * H + SELECTED:2 * KT * H + SELECTED + H1]
        select_f = staging[0:2 * FO, 2 * KT * H:2 * KT * H + SELECTED]
        dense_parts = sb("dense_parts", [3 * GAP, NB], f32r)
        h1 = sb("h1", [128, M1, NB])
        h2 = sb("h2", [128, M2, NB])
        z2 = h2[:, 1, :]
        dense_now = h2[0:3 * GAP, 0, :]
        y = h2[0:1, 1, :]

        rep_ps = [ps(f"rep_ps{n}", [128, COLS]) for n in range(REP_BANKS)]
        x1_ps = [ps(f"x1_ps{n}", [H, COLS]) for n in range(2)]
        aux_ps = ps("aux_ps", [128, 512])
        g_ps = [ps(f"g_ps{n}", [128, QB * FO]) for n in range(2)]
        mlp_ps = ps("mlp_ps", [128, 2, NB])

        consts_loaded = sem("consts_loaded")
        w0_loaded = sem("w0_loaded")
        w1_loaded = sem("w1_loaded")
        dense_loaded = sem("dense_loaded")
        dense_hi_ready = sem("dense_hi_ready")
        dense_split = sem("dense_split")
        zeroed = sem("zeroed")
        wt1_dense_loaded = sem("wt1_dense_loaded")
        wt1_dense_split = sem("wt1_dense_split")
        mlp_loaded = sem("mlp_loaded")
        select_ready = sem("select_ready")
        w0_step = sem("w0_step")
        w0_split = sem("w0_split")
        ids_loaded = [sem(f"ids_loaded{n}") for n in range(2)]
        gathered = [sem(f"gathered{n}") for n in range(2)]
        tiles_begun = sem("tiles_begun")
        e_hi_ready = sem("e_hi_ready")
        split_done = sem("split_done")
        eT_in_ps = sem("eT_in_ps")
        eT_ready = sem("eT_ready")
        cycle_in_ps = sem("cycle_in_ps")
        cycle_ready = sem("cycle_ready")
        left_ready = sem("left_ready")
        rep_in_ps = sem("rep_in_ps")
        shifted_ready = [sem(f"shifted_ready{n}") for n in range(BY_DMA)]
        product_ready = sem("product_ready")
        hi_ready = sem("hi_ready")
        lo_ready = sem("lo_ready")
        contracted = sem("contracted")
        x1_ready = sem("x1_ready")
        e_stored = sem("e_stored")
        e_diag_ready = [sem(f"e_diag_ready{n}") for n in range(2)]
        x1T_in_ps = sem("x1T_in_ps")
        x1T_hi_ready = sem("x1T_hi_ready")
        x1T_lo_ready = sem("x1T_lo_ready")
        g_in_ps = sem("g_in_ps")
        e_diag_free = sem("e_diag_free")
        g_ready = sem("g_ready")
        z2_in_ps = sem("z2_in_ps")
        z2_ready = sem("z2_ready")
        h1_in_ps = sem("h1_in_ps")
        h1_ready = sem("h1_ready")
        h2_in_ps = sem("h2_in_ps")
        h2_ready = sem("h2_ready")
        y_in_ps = sem("y_in_ps")
        y_ready = sem("y_ready")
        y_stored = sem("y_stored")

        block = ctx.enter_context(nc.Block())

        @block.sync
        def _(sp):
            for slot in range(TPI):
                sp.dma_start(ids_sb[slot][:, :], ids[slot * TB:(slot + 1) * TB, :]).then_inc(ids_loaded[slot], 16)
            sp.dma_start(ident[:, :], identity).then_inc(consts_loaded, 16)
            sp.dma_start(select_f, select).then_inc(consts_loaded, 16)
            sp.dma_start(w0_both, w0).then_inc(w0_loaded, 16)
            sp.wait_ge(zeroed, 1)
            for n in range(3):
                sp.dma_start(wt1_dense_f[n * GAP:n * GAP + D, :], w_top1[2 * H:2 * H + D, :]).then_inc(wt1_dense_loaded, 16)
            sp.dma_start(w1T[:, :, :], w1).then_inc(w1_loaded, 16)
            sp.dma_start(wt1_cin[:, :, :], w_top1[0:2 * H, :].rearrange("(k p) n -> p k n", p=128)).then_inc(mlp_loaded, 16)
            sp.dma_start(wt2[:, :, :], w_top2.rearrange("(k p) n -> p k n", p=128)).then_inc(mlp_loaded, 16)
            sp.dma_start(wt3[:, :], w_top3).then_inc(mlp_loaded, 16)
            sp.dma_start(bias1[:, :], b_top1).then_inc(mlp_loaded, 16)
            sp.dma_start(bias2[:, :], b_top2).then_inc(mlp_loaded, 16)

            def store_parts(t, first_row):
                sp.wait_ge(split_done, t + 1)
                sp.dma_start(e_scratch[bass.ds(first_row, TB), :, :], e_parts[:, :, :, :].rearrange("b d q f -> b d (q f)")).then_inc(e_stored, 16)

            def spread(it, c):
                g = it * CPI + c
                if isinstance(it, int) and g == 0:
                    sp.wait_ge(e_stored, 16)
                sp.wait_ge(e_diag_free, g + 1)
                rows = e_scratch[bass.ds(it * NB + c * CB, CB), :, :].rearrange("(q b) d x -> b d q x", b=QB)
                for b in range(QB):
                    sp.dma_start(e_diag[c % 2][b * D:(b + 1) * D, b, :, :, :].rearrange("p q a f -> p q (a f)").bitcast(f32),
                                 rows[b]).then_inc(e_diag_ready[c % 2], 16)

            def rotate(it, c):
                sp.wait_ge(cycle_ready, it * CPI + c + 1)
                for n in range(PER_TILE):
                    start = -n * KT % F
                    sp.dma_start(left[c % 2][n * F:(n + 1) * F, :], cycle[c % 2][start:start + F, :]).then_inc(left_ready, 16)

            def shift_rows(it, c):
                after(sp, product_ready, (it * CPI + c) * KT)
                for k in range(BY_PE, KT):
                    rows = rows_of(k)
                    sp.dma_start(shifted[0:rows, k - BY_PE, :], cycle[c % 2][k:k + rows, :]).then_inc(shifted_ready[k - BY_PE], 16)

            def load_dense(it):
                after(sp, dense_split, it)
                for n in range(3 * GAP // D):
                    sp.dma_start(dense_now[n * D:(n + 1) * D, :], dense_t[:, bass.ds(it * NB, NB)]).then_inc(dense_loaded, 16)

            def store_y(it):
                sp.wait_ge(y_ready, it + 1)
                sp.dma_start(out.rearrange("b o -> o b")[:, bass.ds(it * NB, NB)], y[:, :]).then_inc(y_stored, 16)

            def body(it, first=False, second=False, final=False):
                for c in range(CPI):
                    has_next = not (final and c == CPI - 1)
                    if has_next:
                        rotate(*chunk_after(it, c))
                    spread(it, c)
                    if has_next:
                        shift_rows(*chunk_after(it, c))
                    if c % CPT == 2 and not (final and c >= CPT):
                        store_parts(it * TPI + c // CPT + 1, it * NB + (c // CPT + 1) * TB)
                    if c == 0 and not first and not second:
                        store_y(it - 2)
                    if c == 2 and not first:
                        load_dense(it - 1)
                    if c % CPT == 0 and not final:
                        slot = c // CPT
                        sp.wait_ge(gathered[slot], (it + 1) * (16 * F))
                        sp.dma_start(ids_sb[slot][:, :], ids[bass.ds((it + 1) * NB + slot * TB, TB), :]).then_inc(ids_loaded[slot], 16)

            store_parts(0, 0)
            rotate(0, 0)
            shift_rows(0, 0)
            body(0, first=True)
            body(1, second=True)
            with sp.Fori(2, ITERS - 1) as it:
                body(it)
            body(ITERS - 1, final=True)
            store_y(ITERS - 2)
            load_dense(ITERS - 1)
            store_y(ITERS - 1)
            sp.wait_ge(y_stored, 16 * ITERS)

        @block.gpsimd
        def _(pool):
            def body(it):
                for slot in range(TPI):
                    pool.wait_ge(ids_loaded[slot], it * 16 + 16)
                    after(pool, split_done, (it - 1) * TPI + slot + 1)
                    pool.sem_inc(tiles_begun, 1)
                    for f in range(F):
                        nc.gpsimd.indirect_dma_start(
                            out=e_rows[slot][:, f * D:(f + 1) * D], out_offset=None, in_=tables[f],
                            in_offset=bass.IndirectOffsetOnAxis(ap=ids_sb[slot][:, f:f + 1], axis=0),
                        ).then_inc(gathered[slot], 16)

            body(0)
            with pool.Fori(1, ITERS) as it:
                body(it)

        @block.tensor
        def _(pe):
            def columns(c):
                return eT[c // CPT][:, :, :].rearrange("r b d -> r (b d)")[:, c % CPT * COLS:(c % CPT + 1) * COLS]

            def transpose_e(t, n):
                pe.wait_ge(split_done, t + 1)
                after(pe, eT_ready, t * ET + n)
                for m in range(DPB):
                    last = nc.tensor.transpose(aux_ps[0:2 * FO, m * TB:(m + 1) * TB],
                                               e_parts[:, n * DPB + m, :, :].rearrange("b q f -> b (q f)"), ident[:, :])
                last.then_inc(eT_in_ps, 1)

            def replicate(it, c, item):
                g = it * CPI + c
                if item == 0 and c % CPT == 0:
                    pe.wait_ge(eT_ready, (it * TPI + c // CPT + 1) * ET)
                back, before = rep_before(c, item)
                if before == 0:
                    after(pe, cycle_ready, g - back + 1)
                else:
                    after(pe, product_ready, (g - back) * KT + before + 1)
                rows = rows_of(item) if item else CYCLE
                nc.tensor.matmul(rep_ps[rep_bank(c, item)][0:rows, :], select_r[:, item:item + rows], columns(c),
                                 start=True, stop=True).then_inc(rep_in_ps if item else cycle_in_ps, 1)

            def contract(it, c, k):
                g = it * CPI + c
                if k == 0:
                    after(pe, x1_ready, g - 1)
                pe.wait_ge(hi_ready, g * KT + k + 1)
                rows, slot = rows_of(k), (c * KT + k) % RING
                nc.tensor.matmul(x1_ps[c % 2][:, :], w0_hi[0:rows, k, :], product_hi[0:rows, slot, :], start=(k == 0), stop=False)
                nc.tensor.matmul(x1_ps[c % 2][:, :], w0_lo[0:rows, k, :], product_hi[0:rows, slot, :], start=False, stop=False)
                pe.wait_ge(lo_ready, g * KT + k + 1)
                last = nc.tensor.matmul(x1_ps[c % 2][:, :], w0_hi[0:rows, k, :], product_lo[0:rows, (c * KT + k) % LO_RING, :],
                                        start=False, stop=(k == KT - 1))
                last.then_inc(contracted, 1)

            def transpose_x1(it, c, final=False):
                g = it * CPI + c
                pe.wait_ge(x1_ready, g + 1)
                after(pe, x1T_lo_ready, g)
                if (c % CPT, 0) == (2, 0) and not final:
                    pe.wait_ge(eT_ready, (it * TPI + c // CPT + 2) * ET)
                for q in range(Q):
                    last = nc.tensor.transpose(aux_ps[:, q * 128:(q + 1) * 128], x1[:, q * 128:(q + 1) * 128], ident[:, :])
                last.then_inc(x1T_in_ps, 1)

            def make_g(it, c, q, final=False):
                g = it * CPI + c
                if q == 0:
                    pe.wait_ge(x1T_hi_ready, g + 1)
                    pe.wait_ge(x1T_lo_ready, g + 1)
                    pe.wait_ge(e_diag_ready[c % 2], (it * (CPI // 2) + c // 2 + 1) * (16 * QB))
                after(pe, g_ready, Q * g + q - 1)
                if q == Q - 1 and c % CPT == 2 and not final:
                    pe.wait_ge(e_stored, (it * TPI + c // CPT + 2) * 16)
                for n, (x, part) in enumerate(((x1T_hi, 0), (x1T_hi, 1), (x1T_lo, 0))):
                    last = nc.tensor.matmul(g_ps[q % 2][:, :], x[:, q, :], e_diag[c % 2][:, :, q, part, :],
                                            start=(n == 0), stop=(n == 2))
                last.then_inc(e_diag_free if q == Q - 1 else g_in_ps, 1)

            def layer1(it, fields):
                for j in fields:
                    if j == 0:
                        pe.wait_ge(g_ready, Q * CPI * (it + 1))
                        after(pe, y_ready, it)
                    last = nc.tensor.matmul(mlp_ps[:, 0, :], w1T[:, j, :], G[:, j, bass.ds(it % 2 * NB, NB)],
                                            start=(j == 0), stop=(j == F - 1))
                    if j == F - 1:
                        last.then_inc(z2_in_ps, 1)

            def mlp1(it, third):
                if third == 0:
                    pe.wait_ge(z2_ready, it + 1)
                    pe.wait_ge(dense_split, it + 1)
                if third == 3:
                    pe.wait_ge(h1_ready, it * M1 + 2)
                operands = ((wt1_cin[:, 0, :], G[:, F, bass.ds(it % 2 * NB, NB)]), (wt1_dense[:, :], dense_parts[:, :]),
                            (wt1_cin[:, 1, :], z2[:, :]))
                for n in (2 * third, 2 * third + 1):
                    m, part = n // 3, n % 3
                    weights, x = operands[part]
                    last = nc.tensor.matmul(mlp_ps[:, m % 2, :], weights[:, m * 128:(m + 1) * 128], x,
                                            start=(part == 0), stop=(part == 2))
                if third % 3 == 2:
                    last.then_inc(h1_in_ps, 1)

            def mlp2(it, quarter):
                if quarter == 0:
                    pe.wait_ge(h1_ready, (it + 1) * M1)
                for n in (2 * quarter, 2 * quarter + 1):
                    m, k = n // M1, n % M1
                    last = nc.tensor.matmul(mlp_ps[:, m, :], wt2[:, k, m * 128:(m + 1) * 128], h1[:, k, :],
                                            start=(k == 0), stop=(k == M1 - 1))
                if quarter == 3:
                    last.then_inc(h2_in_ps, 1)

            def mlp3(it):
                pe.wait_ge(h2_ready, (it + 1) * M2)
                for k in range(M2):
                    last = nc.tensor.matmul(mlp_ps[0:1, 0, :], wt3[:, k:k + 1], h2[:, k, :], start=(k == 0), stop=(k == M2 - 1))
                last.then_inc(y_in_ps, 1)

            def chunk(it, c, first=False, second=False, final=False):
                has_last = not (first and c == 0)
                has_next = not (final and c == CPI - 1)
                next_tile = it * TPI + c // CPT + 1
                makes_eT = not (final and c >= CPT)
                last = chunk_before(it, c)
                for k in range(KT):
                    for item in ITEMS_AT[k]:
                        if item < REPS:
                            replicate(it, c, item)
                        elif has_next:
                            replicate(*chunk_after(it, c), item - REPS)
                    if makes_eT and (c % CPT, k) in ET_STEPS:
                        if (c % CPT, k) == ET_STEPS[0]:
                            after(pe, x1T_lo_ready, it * CPI + c)
                        transpose_e(next_tile, ET_STEPS.index((c % CPT, k)))
                    if has_last:
                        if k == 1:
                            transpose_x1(*last, final and c >= CPT)
                        if k >= KT - Q:
                            make_g(*last, k - (KT - Q), final and c >= CPT)
                    if not first:
                        layer1(it - 1, fields_at(c, k))
                        if (c, k) in MLP1_STEPS:
                            mlp1(it - 1, MLP1_STEPS.index((c, k)))
                    if not first and not second:
                        if (c, k) in MLP2_STEPS:
                            mlp2(it - 2, MLP2_STEPS.index((c, k)))
                        if (c, k) == MLP3_STEP:
                            mlp3(it - 2)
                    contract(it, c, k)

            pe.wait_ge(consts_loaded, 32)
            for n in range(ET):
                transpose_e(0, n)
            pe.wait_ge(select_ready, 1)
            pe.wait_ge(w0_split, 2)
            for item in range(ITEMS_AT[0][0]):
                replicate(0, 0, item)
            for c in range(CPI):
                chunk(0, c, first=True)
            pe.wait_ge(w1_loaded, 16)
            pe.wait_ge(wt1_dense_split, 2)
            pe.wait_ge(mlp_loaded, 5 * 16)
            for c in range(CPI):
                chunk(1, c, second=True)
            with pe.Fori(2, ITERS - 1) as it:
                for c in range(CPI):
                    chunk(it, c)
            end = ITERS - 1
            for c in range(CPI):
                chunk(end, c, final=True)
            for n in range(len(MLP2_STEPS)):
                mlp2(end - 1, n)
            transpose_x1(end, CPI - 1)
            mlp3(end - 1)
            for q in range(Q):
                make_g(end, CPI - 1, q)
            layer1(end, range(F))
            for n in range(len(MLP1_STEPS)):
                mlp1(end, n)
            for n in range(len(MLP2_STEPS)):
                mlp2(end, n)
            mlp3(end)

        @block.scalar
        def _(act):
            def copy_eT(slot, t, n):
                act.wait_ge(eT_in_ps, t * ET + n + 1)
                nc.scalar.copy(eT[slot][:, :, n * DPB:(n + 1) * DPB].rearrange("r b d -> r d b"),
                               aux_ps[0:2 * FO, :].rearrange("r (d b) -> r d b", b=TB)).then_inc(eT_ready, 1)

            def copy_cycle(it, c):
                g = it * CPI + c
                act.wait_ge(cycle_in_ps, g + 1)
                nc.scalar.copy(cycle[c % 2][:, :], rep_ps[rep_bank(c, 0)][0:CYCLE, :]).then_inc(cycle_ready, 1)

            def round_product(it, c, k):
                g = it * CPI + c
                act.wait_ge(product_ready, g * KT + k + 1)
                after(act, contracted, g * KT + k + 1 - held_in_slot(c, k))
                n, rows = c * KT + k, rows_of(k)
                nc.scalar.copy(product_hi[0:rows, n % RING, :], products[0:rows, n % RING, :]).then_inc(hi_ready, 1)

            def copy_x1(it, c):
                act.wait_ge(contracted, (it * CPI + c + 1) * KT)
                nc.scalar.copy(x1[:, :], x1_ps[c % 2][:, :]).then_inc(x1_ready, 1)

            def round_x1T(it, c):
                act.wait_ge(x1T_in_ps, it * CPI + c + 1)
                nc.scalar.copy(x1T_hi[:, :, :].rearrange("p q i -> p (q i)"), aux_ps[:, :]).then_inc(x1T_hi_ready, 1)

            def copy_g(it, c, q):
                if q == Q - 1:
                    act.wait_ge(e_diag_free, it * CPI + c + 3)
                else:
                    act.wait_ge(g_in_ps, (it * CPI + c) * (Q - 1) + q + 1)
                nc.scalar.copy(G[:, :, bass.ds(it % 2 * NB + c * CB + q * QB, QB)].rearrange("i f b -> i b f"),
                               g_ps[q % 2][:, :].rearrange("i (b f) -> i b f", f=FO)).then_inc(g_ready, 1)

            def copy_z2(it):
                after(act, y_stored, 16 * it)
                act.wait_ge(z2_in_ps, it + 1)
                nc.scalar.copy(z2[:, :], mlp_ps[:, 0, :]).then_inc(z2_ready, 1)

            def round_dense(it):
                act.wait_ge(dense_loaded, (it + 1) * (16 * 3 * GAP // D))
                nc.scalar.copy(dense_parts[:, :], dense_now[:, :]).then_inc(dense_hi_ready, 1)

            def relu1(it, pair):
                act.wait_ge(h1_in_ps, it * 2 + pair + 1)
                for m in (2 * pair, 2 * pair + 1):
                    nc.scalar.activation(h1[:, m, :], mlp_ps[:, m % 2, :], ACT.Relu, bias=bias1[:, m:m + 1]).then_inc(h1_ready, 1)

            def relu2(it):
                act.wait_ge(h2_in_ps, it + 1)
                for m in range(M2):
                    nc.scalar.activation(h2[:, m, :], mlp_ps[:, m, :], ACT.Relu, bias=bias2[:, m:m + 1]).then_inc(h2_ready, 1)

            def copy_y(it):
                act.wait_ge(y_in_ps, it + 1)
                nc.scalar.copy(y[:, :], mlp_ps[0:1, 0, :]).then_inc(y_ready, 1)

            def chunk(it, c, first=False, second=False, final=False):
                has_last = not (first and c == 0)
                has_next = not (final and c == CPI - 1)
                next_tile = it * TPI + c // CPT + 1
                makes_eT = not (final and c >= CPT)
                last = chunk_before(it, c)
                for k in range(KT):
                    if k + 1 < KT:
                        round_product(it, c, k + 1)
                    elif has_next:
                        round_product(*chunk_after(it, c), 0)
                    if k == 0 and has_last:
                        copy_x1(*last)
                    if REPS in ITEMS_AT[k] and has_next:
                        copy_cycle(*chunk_after(it, c))
                    c1, k1 = (c, k - 1) if k else (c - 1, KT - 1)
                    if makes_eT and (c % CPT, k) in ET_STEPS:
                        copy_eT((c // CPT + 1) % TPI, next_tile, ET_STEPS.index((c % CPT, k)))
                    if k > KT - Q and has_last:
                        copy_g(*last, k1 - (KT - Q))
                    if k == 0 and not (first and c <= 1):
                        copy_g(*chunk_before(*last), Q - 1)
                    if not first and c1 >= 0:
                        if len(fields_at(c1, k1)) and fields_at(c1, k1)[-1] == F - 1:
                            copy_z2(it - 1)
                        if (c1, k1) in MLP1_STEPS[2::3]:
                            relu1(it - 1, MLP1_STEPS[2::3].index((c1, k1)))
                    if not first and not second and (c1, k1) == MLP2_STEPS[-1]:
                        relu2(it - 2)
                    if k == 1 and has_last:
                        round_x1T(*last)
                    if (c, k) == DENSE_STEP and not first:
                        round_dense(it - 1)
                    if (c, k) == MLP3_STEP and not first and not second:
                        copy_y(it - 2)

            for n in range(ET):
                copy_eT(0, 0, n)
            act.wait_ge(mlp_loaded, 5 * 16)
            copy_cycle(0, 0)
            round_product(0, 0, 0)
            for c in range(CPI):
                chunk(0, c, first=True)
            for c in range(CPI):
                chunk(1, c, second=True)
            with act.Fori(2, ITERS - 1) as it:
                for c in range(CPI):
                    chunk(it, c)
            end = ITERS - 1
            for c in range(CPI):
                chunk(end, c, final=True)
            copy_x1(end, CPI - 1)
            copy_g(end, CPI - 2, Q - 1)
            relu2(end - 1)
            round_x1T(end, CPI - 1)
            copy_y(end - 1)
            for q in range(Q):
                copy_g(end, CPI - 1, q)
            round_dense(end)
            copy_z2(end)
            for pair in range(M1 // 2):
                relu1(end, pair)
            relu2(end)
            copy_y(end)

        @block.vector
        def _(dve):
            nc.vector.memset(wt1_dense_f, 0.0).then_inc(zeroed, 1)
            dve.wait_ge(consts_loaded, 32)
            nc.vector.tensor_copy(select_r[:, :], select_f).then_inc(select_ready, 1)
            for n in range(2):
                nc.vector.memset(e_diag[n][:, :, :, :, :].bitcast(f32), 0.0).then_inc(e_diag_free, 1)
            nc.vector.memset(e_parts[:, :, 0, F], 1.0)
            nc.vector.memset(e_parts[:, :, 1, F], 0.0)
            dve.wait_ge(w0_loaded, 16)
            nc.vector.memset(w0_both[0:F, 1, 0, :], 0.0).then_inc(w0_step, 1)
            dve.wait_ge(w0_step, 1)
            nc.vector.tensor_tensor(w0_sum, w0_sum, w0_both[:, 1, :, :], ALU.add).then_inc(w0_step, 1)
            dve.wait_ge(w0_step, 2)
            nc.vector.tensor_copy(w0_hi[:, :, :], w0_sum).then_inc(w0_split, 1)
            dve.wait_ge(w0_split, 1)
            nc.vector.tensor_tensor(w0_lo[:, :, :], w0_sum, w0_hi[:, :, :].bitcast(f32), ALU.subtract).then_inc(w0_split, 1)
            dve.wait_ge(wt1_dense_loaded, 48)
            nc.vector.tensor_copy(wt1_dense[:, :], wt1_dense_f).then_inc(wt1_dense_split, 1)
            dve.wait_ge(wt1_dense_split, 1)
            nc.vector.tensor_tensor(wt1_dense[2 * GAP:3 * GAP, :], wt1_dense_f[2 * GAP:3 * GAP, :],
                                    wt1_dense[2 * GAP:3 * GAP, :].bitcast(f32), ALU.subtract).then_inc(wt1_dense_split, 1)

            def split_hi(t, it, slot):
                dve.wait_ge(gathered[slot], (it + 1) * (16 * F))
                after(dve, eT_in_ps, ET * t)
                after(dve, e_stored, 16 * t)
                nc.vector.tensor_copy(e_parts[:, :, 0, 0:F].bitcast(f32r),
                                      e_rows[slot][:, :].rearrange("b (f d) -> b d f", d=D)).then_inc(e_hi_ready, 1)

            def split_lo(t, slot):
                dve.wait_ge(e_hi_ready, t + 1)
                nc.vector.tensor_tensor(e_parts[:, :, 1, 0:F], e_rows[slot][:, :].rearrange("b (f d) -> b d f", d=D),
                                        e_parts[:, :, 0, 0:F], ALU.subtract).then_inc(split_done, 1)

            def multiply(it, c, k):
                g = it * CPI + c
                n, rows = c * KT + k, rows_of(k)
                if k == 0:
                    dve.wait_ge(left_ready, (g + 1) * (16 * PER_TILE))
                    x = cycle[c % 2]
                elif k < BY_PE:
                    dve.wait_ge(rep_in_ps, g * (BY_PE - 1) + k)
                    x = rep_ps[rep_bank(c, k)]
                else:
                    dve.wait_ge(shifted_ready[k - BY_PE], (g + 1) * 16)
                    x = shifted[:, k - BY_PE, :]
                after(dve, lo_ready, g * KT + k + 1 - held_in_slot(c, k))
                nc.vector.tensor_tensor(products[0:rows, n % RING, :], x[0:rows, :],
                                        left[c % 2][0:rows, :], ALU.mult).then_inc(product_ready, 1)

            def lower_part(it, c, k):
                g = it * CPI + c
                n, rows = c * KT + k, rows_of(k)
                dve.wait_ge(hi_ready, g * KT + k + 1)
                after(dve, contracted, g * KT + k + 1 - LO_RING)
                nc.vector.tensor_tensor(product_lo[0:rows, n % LO_RING, :], products[0:rows, n % RING, :],
                                        product_hi[0:rows, n % RING, :].bitcast(f32), ALU.subtract).then_inc(lo_ready, 1)

            def lower_dense(it):
                dve.wait_ge(dense_hi_ready, it + 1)
                nc.vector.tensor_tensor(dense_parts[GAP:2 * GAP, :], dense_now[GAP:2 * GAP, :],
                                        dense_parts[GAP:2 * GAP, :].bitcast(f32), ALU.subtract).then_inc(dense_split, 1)

            def lower_x1T(it, c):
                dve.wait_ge(x1T_hi_ready, it * CPI + c + 1)
                nc.vector.tensor_tensor(x1T_lo[:, :, :].rearrange("p q i -> p (q i)"), aux_ps[:, :],
                                        x1T_hi[:, :, :].rearrange("p q i -> p (q i)").bitcast(f32),
                                        ALU.subtract).then_inc(x1T_lo_ready, 1)

            def chunk(it, c, first=False, final=False):
                has_last = not (first and c == 0)
                has_next = not (final and c == CPI - 1)
                last = chunk_before(it, c)
                for k in range(KT):
                    if k + 1 < KT:
                        multiply(it, c, k + 1)
                    elif has_next:
                        multiply(*chunk_after(it, c), 0)
                    lower_part(it, c, k)
                    if k == 2 and has_last:
                        lower_x1T(*last)
                    if (c, k - 2) == DENSE_STEP and not first:
                        lower_dense(it - 1)
                    if c == 2 and k == 1:
                        split_hi(it * TPI + 1, it, 1)
                    if c == 2 and k == 2:
                        split_lo(it * TPI + 1, 1)
                    if c == CPT + 2 and k == 1 and not final:
                        split_hi(it * TPI + 2, it + 1, 0)
                    if c == CPT + 2 and k == 2 and not final:
                        split_lo(it * TPI + 2, 0)

            split_hi(0, 0, 0)
            split_lo(0, 0)
            multiply(0, 0, 0)
            for c in range(CPI):
                chunk(0, c, first=True)
            with dve.Fori(1, ITERS - 1) as it:
                for c in range(CPI):
                    chunk(it, c)
            end = ITERS - 1
            for c in range(CPI):
                chunk(end, c, final=True)
            lower_x1T(end, CPI - 1)
            lower_dense(end)


_INS = ["dense_ctx", "ids"] + [f"tbl_{f}" for f in range(F)] + [
    "W_top1", "b_top1", "W_top2", "b_top2", "W_top3", "L0_rec_W0", "L0_rec_W1"]


def _constants():
    copies = np.zeros((2, FO, CYCLE), np.float32)
    copies[:, np.arange(CYCLE) % F, np.arange(CYCLE)] = 1.0
    return {"select": copies.reshape(2 * FO, -1), "identity": np.eye(128, dtype=np.float32)}


def kernel(**inputs):
    import concourse.bacc as _bacc
    from concourse.bass_utils import run_bass_kernel_spmd as _run

    nc = _bacc.Bacc("TRN2", target_bir_lowering=False, num_devices=1)
    arrays, aps = {}, {}
    given = {name: np.ascontiguousarray(inputs[name]) for name in _INS}
    given.update(_constants())
    w0 = given["L0_rec_W0"].reshape(H, F, F)
    tile, row = np.divmod(np.arange(KT * ROWS), ROWS)
    block, field = np.divmod(row, F)
    j, k = (field - block * KT) % F, (field + tile) % F
    both = np.stack([w0[:, j, k], w0[:, k, j]])
    given["L0_rec_W0"] = np.ascontiguousarray(both.reshape(2, H, KT, ROWS).transpose(3, 0, 2, 1))
    given["L0_rec_W1"] = np.ascontiguousarray(given["L0_rec_W1"].reshape(H, H, F).transpose(1, 2, 0))
    given["dense_ctx"] = np.ascontiguousarray(given["dense_ctx"].T)
    for name in ("b_top1", "b_top2", "W_top3"):
        given[name] = np.ascontiguousarray(given[name].reshape(-1, 128).T)
    for name, a in given.items():
        arrays[f"in_{name}_dram"] = a
        aps[name] = nc.dram_tensor(f"in_{name}_dram", a.shape, mybir.dt.from_np(a.dtype), kind="ExternalInput").ap()
    out = nc.dram_tensor("out_0_dram", (B, 1), mybir.dt.float32, kind="ExternalOutput").ap()
    e_scratch = nc.dram_tensor("e_scratch", (B, D, 2 * FO), mybir.dt.float32, kind="Internal").ap()
    cin_tower(nc, aps["dense_ctx"], aps["ids"], [aps[f"tbl_{f}"] for f in range(F)], aps["W_top1"], aps["b_top1"],
              aps["W_top2"], aps["b_top2"], aps["W_top3"], aps["L0_rec_W0"], aps["L0_rec_W1"],
              aps["select"], aps["identity"], e_scratch, out)
    r = _run(nc, [arrays], core_ids=[0])
    return r.results[0]["out_0_dram"]
```
